# Optimizing a Trainium2 kernel written in Bass

```python
import numpy as np
import jax
import jax.numpy as jnp

def _softmax(x, axis=-1):
    return jax.nn.softmax(x, axis=axis)

def _gelu(x):
    return jax.nn.gelu(x, approximate=True)

def _silu(x):
    return jax.nn.silu(x)

def _sigmoid(x):
    return jax.nn.sigmoid(x)

def _layernorm(x, axis=-1, eps=1e-05):
    m = jnp.mean(x, axis=axis, keepdims=True)
    v = jnp.var(x, axis=axis, keepdims=True)
    return (x - m) / jnp.sqrt(v + eps)

def _scatter_add(tgt, idx, src, axis=0):
    return tgt.at[idx].add(src)

def _segment_sum(src, seg, n):
    return jax.ops.segment_sum(src, seg, n)
kernel_name = 'mk_cond_resid_d4_seqx_r8_d8b294'

def setup_inputs(seed: int=0):
    np.random.seed(seed)
    _w = jnp.asarray

    def _rec_inputs():
        import jax
        import jax.numpy as jnp
        _rk = jax.random.key(seed)
        x = -0.0002071 + 1 * jax.random.normal(jax.random.fold_in(_rk, 1), (8, 128, 128), jnp.float32)
        _lenS = 128 - jax.random.randint(jax.random.fold_in(_rk, 7), (8,), 0, max(1, 128 // 4) + 1, jnp.int32)
        _lenS2 = 128 - jax.random.randint(jax.random.fold_in(_rk, 8), (8,), 0, max(1, 128 // 4) + 1, jnp.int32)
        cond_8 = jax.random.uniform(jax.random.fold_in(_rk, 11), (8, 8), jnp.float32, 0.0, 0.983423)
        return (x, cond_8)
    x, cond_8 = _rec_inputs()

    def _L0_cond_setup():
        import jax, jax.numpy as jnp
        import numpy as np
        R = 16
        ALPHA = 32.0
        SCALING = ALPHA / R
        key = jax.random.key(seed)
        ks = jax.random.split(key, 6)
        B, T, C, O, E = (16, 1500, 128, 128, 8)
        x = jax.random.normal(ks[0], (B, T, C), dtype=jnp.float32)
        w = jax.random.uniform(ks[1], (B, E), dtype=jnp.float32)
        W_base = jax.random.normal(ks[2], (O, C), dtype=jnp.float32) * 0.02
        b_base = jax.random.normal(ks[3], (O,), dtype=jnp.float32) * 0.02
        As = jax.random.normal(ks[4], (E, R, C), dtype=jnp.float32) * 0.02
        Bs = jax.random.normal(ks[5], (E, O, R), dtype=jnp.float32) * 0.02
        return {'x': x, 'w': w, 'W_base': W_base, 'b_base': b_base, 'As': As, 'Bs': Bs}
    _L0_cond_all = _L0_cond_setup()
    _L0_cond_in = {k: v for k, v in _L0_cond_all.items() if k in ('W_base', 'b_base', 'As', 'Bs')}
    del _L0_cond_all

    def _L1_cond_setup():
        import jax, jax.numpy as jnp
        import numpy as np
        key = jax.random.key(seed)
        k1, k2, k3, k4, k5 = jax.random.split(key, 5)
        B, N, T, O, G = (32, 32, 128, 128, 8)
        x = jax.random.normal(k1, (B, N, T), dtype=jnp.float32)
        y = jax.random.uniform(k2, (B, G), dtype=jnp.float32)
        weight = jax.random.normal(k3, (G, O, T), dtype=jnp.float32) * (1.0 / np.sqrt(T))
        mask = jax.random.uniform(k4, (O, T), dtype=jnp.float32)
        bias = jax.random.normal(k5, (O,), dtype=jnp.float32)
        return {'x': x, 'y': y, 'weight': weight, 'mask': mask, 'bias': bias}
    _L1_cond_all = _L1_cond_setup()
    _L1_cond_in = {k: v for k, v in _L1_cond_all.items() if k in ('weight', 'mask', 'bias')}
    del _L1_cond_all

    def _L2_cond_setup():
        import jax, jax.numpy as jnp
        import numpy as np
        TOP_K = 2
        NUM_MOE_LAYERS = 12

        def _gemma_mlp(x, gate_w, up_w, down_w):
            g = jnp.einsum('bsh,hi->bsi', x, gate_w)
            u = jnp.einsum('bsh,hi->bsi', x, up_w)
            return jnp.einsum('bsi,ih->bsh', jax.nn.gelu(g, approximate=True) * u, down_w)
        key = jax.random.key(seed)
        ks = jax.random.split(key, 8)
        B, S, H, I, E = (32, 32, 128, 512, 8)
        std = 0.02
        return {'x': jax.random.normal(ks[0], (B, S, H), jnp.float32), 'router_logits': jax.random.normal(ks[1], (B, E), jnp.float32), 'skill_gate': jax.random.normal(ks[2], (E, H, I), jnp.float32) * std, 'skill_up': jax.random.normal(ks[3], (E, H, I), jnp.float32) * std, 'skill_down': jax.random.normal(ks[4], (E, I, H), jnp.float32) * std, 'shared_gate': jax.random.normal(ks[5], (H, I), jnp.float32) * std, 'shared_up': jax.random.normal(ks[6], (H, I), jnp.float32) * std, 'shared_down': jax.random.normal(ks[7], (I, H), jnp.float32) * std}
    _L2_cond_all = _L2_cond_setup()
    _L2_cond_in = {k: v for k, v in _L2_cond_all.items() if k in ('skill_gate', 'skill_up', 'skill_down', 'shared_gate', 'shared_up', 'shared_down')}
    del _L2_cond_all

    def _L3_cond_setup():
        import jax, jax.numpy as jnp
        import numpy as np
        B, S, D = (16, 256, 128)
        E, H = (8, 256)
        key = jax.random.key(seed)
        ks = jax.random.split(key, 8)
        scale = 0.02
        x = jax.random.normal(ks[0], (B, S, D), dtype=jnp.float32)
        opcode_onehot = jax.random.uniform(ks[1], (B, E), dtype=jnp.float32)
        W_up = jax.random.normal(ks[2], (E, H, D), dtype=jnp.float32) * scale
        b_up = jnp.zeros((E, H), dtype=jnp.float32)
        W_gate = jax.random.normal(ks[3], (E, H, D), dtype=jnp.float32) * scale
        b_gate = jnp.zeros((E, H), dtype=jnp.float32)
        W_down = jax.random.normal(ks[4], (E, D, H), dtype=jnp.float32) * scale
        b_down = jnp.zeros((E, D), dtype=jnp.float32)
        return {'x': x, 'opcode_onehot': opcode_onehot, 'W_up': W_up, 'b_up': b_up, 'W_gate': W_gate, 'b_gate': b_gate, 'W_down': W_down, 'b_down': b_down}
    _L3_cond_all = _L3_cond_setup()
    _L3_cond_in = {k: v for k, v in _L3_cond_all.items() if k in ('W_up', 'b_up', 'W_gate', 'b_gate', 'W_down', 'b_down')}
    del _L3_cond_all
    return {'x': x, 'cond_8': cond_8, 'L0_cond_W_base': _L0_cond_in['W_base'], 'L0_cond_b_base': _L0_cond_in['b_base'], 'L0_cond_As': _L0_cond_in['As'], 'L0_cond_Bs': _L0_cond_in['Bs'], 'L1_cond_weight': _L1_cond_in['weight'], 'L1_cond_mask': _L1_cond_in['mask'], 'L1_cond_bias': _L1_cond_in['bias'], 'L2_cond_skill_gate': _L2_cond_in['skill_gate'], 'L2_cond_skill_up': _L2_cond_in['skill_up'], 'L2_cond_skill_down': _L2_cond_in['skill_down'], 'L2_cond_shared_gate': _L2_cond_in['shared_gate'], 'L2_cond_shared_up': _L2_cond_in['shared_up'], 'L2_cond_shared_down': _L2_cond_in['shared_down'], 'L3_cond_W_up': _L3_cond_in['W_up'], 'L3_cond_b_up': _L3_cond_in['b_up'], 'L3_cond_W_gate': _L3_cond_in['W_gate'], 'L3_cond_b_gate': _L3_cond_in['b_gate'], 'L3_cond_W_down': _L3_cond_in['W_down'], 'L3_cond_b_down': _L3_cond_in['b_down']}

def reference(x, cond_8, L0_cond_W_base, L0_cond_b_base, L0_cond_As, L0_cond_Bs, L1_cond_weight, L1_cond_mask, L1_cond_bias, L2_cond_skill_gate, L2_cond_skill_up, L2_cond_skill_down, L2_cond_shared_gate, L2_cond_shared_up, L2_cond_shared_down, L3_cond_W_up, L3_cond_b_up, L3_cond_W_gate, L3_cond_b_gate, L3_cond_W_down, L3_cond_b_down):
    import jax
    import jax.numpy as jnp

    def _L0_cond_ref(x, w, W_base, b_base, As, Bs):
        import jax, jax.numpy as jnp
        import numpy as np
        R = 16
        ALPHA = 32.0
        SCALING = ALPHA / R
        out = jnp.einsum('btc,oc->bto', x, W_base) + b_base
        h = jnp.einsum('btc,erc->bter', x, As)
        lora = jnp.einsum('bter,eor,be->bto', h, Bs, w)
        return out + lora * SCALING

    def _L1_cond_ref(x, y, weight, mask, bias):
        import jax, jax.numpy as jnp
        import numpy as np
        masked_w = weight * mask[None, :, :]
        w_bot = jnp.einsum('bg,got->bot', y, masked_w)
        return jnp.einsum('bnt,bot->bno', x, w_bot) + bias

    def _L2_cond_ref(x, router_logits, skill_gate, skill_up, skill_down, shared_gate, shared_up, shared_down):
        import jax, jax.numpy as jnp
        import numpy as np
        TOP_K = 2
        NUM_MOE_LAYERS = 12

        def _gemma_mlp(x, gate_w, up_w, down_w):
            g = jnp.einsum('bsh,hi->bsi', x, gate_w)
            u = jnp.einsum('bsh,hi->bsi', x, up_w)
            return jnp.einsum('bsi,ih->bsh', jax.nn.gelu(g, approximate=True) * u, down_w)
        B = x.shape[0]
        E = skill_gate.shape[0]
        rw = jax.nn.softmax(router_logits.astype(jnp.float32), axis=-1)
        w, sel = jax.lax.top_k(rw, TOP_K)
        w = w / w.sum(axis=-1, keepdims=True)
        w = w.astype(x.dtype)
        scale = 1.0 / NUM_MOE_LAYERS
        w = scale * w + (1.0 - scale) * jax.lax.stop_gradient(w)
        dense_w = jnp.zeros((B, E), x.dtype).at[jnp.arange(B)[:, None], sel].add(w)

        def step(acc, params):
            g, u, d, we = params
            return (acc + we[:, None, None] * _gemma_mlp(x, g, u, d), None)
        out, _ = jax.lax.scan(step, jnp.zeros_like(x), (skill_gate, skill_up, skill_down, dense_w.T))
        out = out + _gemma_mlp(x, shared_gate, shared_up, shared_down)
        return out

    def _L3_cond_ref(x, opcode_onehot, W_up, b_up, W_gate, b_gate, W_down, b_down):
        import jax, jax.numpy as jnp
        import numpy as np
        B, S, D = (16, 256, 128)
        E, H = (8, 256)
        expert = jnp.argmax(opcode_onehot, axis=-1)
        wu, bu = (W_up[expert], b_up[expert])
        wg, bg = (W_gate[expert], b_gate[expert])
        wd, bd = (W_down[expert], b_down[expert])
        up = jnp.einsum('bsd,bhd->bsh', x, wu) + bu[:, None, :]
        gate = jnp.einsum('bsd,bhd->bsh', x, wg) + bg[:, None, :]
        hidden = jax.nn.silu(up) * gate
        out = jnp.einsum('bsh,bdh->bsd', hidden, wd) + bd[:, None, :]
        return out
    x = x + _L0_cond_ref(x, cond_8, L0_cond_W_base, L0_cond_b_base, L0_cond_As, L0_cond_Bs)
    x = x + _L1_cond_ref(x, cond_8, L1_cond_weight, L1_cond_mask, L1_cond_bias)
    x = x + _L2_cond_ref(x, cond_8, L2_cond_skill_gate, L2_cond_skill_up, L2_cond_skill_down, L2_cond_shared_gate, L2_cond_shared_up, L2_cond_shared_down)
    x = x + _L3_cond_ref(x, cond_8, L3_cond_W_up, L3_cond_b_up, L3_cond_W_gate, L3_cond_b_gate, L3_cond_W_down, L3_cond_b_down)
    return x

_drawn_inputs = setup_inputs


def setup_inputs(seed=0):
    import zlib

    import numpy as np

    out = dict(_drawn_inputs(seed))
    spreads = {'L3_cond_b_up': (0.0, 0.8), 'L3_cond_b_gate': (0.0, 0.8), 'L3_cond_b_down': (0.0, 0.352)}
    factors = {'L0_cond_b_base': 3.58,
     'L2_cond_skill_gate': 3.635,
     'L2_cond_skill_up': 3.565,
     'L2_cond_skill_down': 3.48,
     'L2_cond_shared_gate': 2.752,
     'L2_cond_shared_down': 2.701,
     'L3_cond_W_up': 3.821,
     'L3_cond_W_gate': 3.789,
     'L3_cond_W_down': 3.702}
    for name, (base, spread) in spreads.items():
        noise = np.random.default_rng([zlib.crc32(name.encode()), seed]).standard_normal(out[name].shape)
        drawn = base * np.exp(spread * noise) if base else spread * noise
        out[name] = jnp.asarray(drawn.astype(out[name].dtype))
    for name, factor in factors.items():
        out[name] = (out[name] * factor).astype(out[name].dtype)
    return out
```

```python
import concourse.bass as bass
from concourse import mybir
from contextlib import ExitStack

B, S, C = 8, 128, 128
E = 8
R = 16
I = 512
H = 256
T = I // 128
HC = H // 128
OL = E * C // 128
OH = C // OL
HALF = B // 2
N = HALF * S
TOP_K = 2
SCALING = 32.0 / R
STOP_SCALE = 1.0 / 12
NSH = 2 * T
LOWEST = -3.0e38


def build(nc, x, cond, w_base, b_base, a_s, b_s, w1, mask, bias1, sk_gate, sk_up, sk_down,
          sh_gate, sh_up, sh_down, w_up, b_up, w_gate, b_gate, w_down, b_down, out):
    fp32, i32 = mybir.dt.float32, mybir.dt.int32
    ALU, ACT, AX = mybir.AluOpType, mybir.ActivationFunctionType, mybir.AxisListType

    ctx = ExitStack()
    with ctx:
        ctx.enter_context(nc.allow_non_contiguous_dma(reason="columns of biases"))

        def sb(name, shape, dt=fp32):
            return ctx.enter_context(nc.sbuf_tensor(name, shape, dt))

        def sem(name):
            return ctx.enter_context(nc.semaphore(name))

        ident = sb("ident", [128, 128])
        seg = sb("seg", [128, E])
        delta = sb("delta", [128, OH])
        rev = sb("rev", [128, E])
        revp = sb("revp", [E, 1])
        condb = sb("condb", [128, B * E])
        segcond = sb("segcond", [128, B, E])
        wcol = sb("wcol", [128, B])
        wcol2 = sb("wcol2", [128, B])
        mix1 = sb("mix1", [128, B, OH])
        m1 = sb("m1", [128, B])
        m2 = sb("m2", [128, B])
        eq = sb("eq", [128, B, E])
        val = sb("val", [128, B, E])
        rank = sb("rank", [128, TOP_K, B])
        hot1 = sb("hot1", [128, B, E])
        hot2 = sb("hot2", [128, B, E])
        rest = sb("rest", [128, B, E])
        chosen = sb("chosen", [128, B * TOP_K], i32)
        shifted = sb("shifted", [128, B, E])
        expo = sb("expo", [128, B, E])
        total = sb("total", [128, B])
        rtotal = sb("rtotal", [128, B])
        prob = sb("prob", [128, B, E])
        picked = sb("picked", [128, B, E])
        pk = sb("pk", [128, B, TOP_K])
        pksum = sb("pksum", [128, B])
        rpksum = sb("rpksum", [128, B])
        wnorm = sb("wnorm", [128, B, TOP_K])
        wpart = sb("wpart", [128, B, TOP_K])
        wsel = sb("wsel", [128, B * TOP_K])
        hot_t = sb("hot_t", [E, B])

        x_in = sb("x_in", [S, B, C])
        small = sb("small", [128, 4, 128])
        small_t = sb("small_t", [128, 4, 128])
        base_t, a_t, b_t, mask_t = (small_t[:, n, :] for n in range(4))
        b0col = sb("b0col", [C, 1])
        b1col = sb("b1col", [C, 1])
        w1_sb = sb("w1_sb", [128, OL, C])
        p1 = sb("p1", [C, B, C])
        lora = sb("lora", [128, B * S])
        x_t = sb("x_t", [C, B * S])
        x1_t = sb("x1_t", [C, B * S])
        x2_t = sb("x2_t", [C, B * S])
        x2s = sb("x2s", [C, B * S])
        shg = sb("shg", [128, I])
        shu = sb("shu", [128, I])
        shd = sb("shd", [128, T, C])
        gate_w = sb("gate_w", [128, 2 * TOP_K, I])
        up_w = sb("up_w", [128, 2 * TOP_K, I])
        down_w = sb("down_w", [128, 2 * TOP_K, T, C])
        gelu = sb("gelu", [128, 2, N])
        hid = sb("hid", [128, 2, N])
        w3 = sb("w3", [128, 2, 3, H])
        w3_t = sb("w3_t", [128, 3, HC, 128])
        bias3 = sb("bias3", [E, 2 * H + C])
        bsel = sb("bsel", [128, 2 * HC + 1, B])
        bhalf = sb("bhalf", [128, HC, B])
        x3_t = sb("x3_t", [C, 2, S])
        x3b_t = sb("x3b_t", [C, 2, S])
        tanh3 = sb("tanh3", [128, HC, S])
        sig3 = sb("sig3", [128, HC, S])
        gsig3 = sb("gsig3", [128, HC, S])
        hid3 = sb("hid3", [128, HC, S])
        out_sb = sb("out_sb", [S, 2, C])

        bank = [ctx.enter_context(nc.psum_tensor(f"bank{n}", [128, 512], fp32)) for n in range(8)]
        g_ps, u_ps = bank[0:2], bank[2:4]
        acc_ps = bank[4]
        sh_acc = [bank[5], bank[7]]
        w3a_ps, w3b_ps = bank[5], bank[6]
        out_ps = bank[6]
        ug3_ps = bank[7]

        cond_in, small_in, bias_in, bias3_in = sem("cond_in"), sem("small_in"), sem("bias_in"), sem("bias3_in")
        x_loaded = [sem("x_loaded0"), sem("x_loaded1")]
        w1_in, sh_in, shd_in = sem("w1_in"), sem("sh_in"), sem("shd_in")
        pair_in = [sem(f"pair_in{n}") for n in range(2 * TOP_K)]
        w3_in = [sem(f"w3_in{n}") for n in range(2)]
        stored = [sem(f"stored{n}") for n in range(2)]
        pool_step = sem("pool_step")
        consts = sem("consts")
        dve_step = sem("dve_step")
        mix_ready, routed, shifted_ready, expo_ready = sem("mix_ready"), sem("routed"), sem("shifted_ready"), sem("expo_ready")
        hot_ready, bias_sel, bsel_ready = sem("hot_ready"), sem("bias_sel"), sem("bsel_ready")
        xt_done, xt_ready = sem("xt_done"), sem("xt_ready")
        smallt_done, smallt_ready = sem("smallt_done"), sem("smallt_ready")
        lora_done, lora_ready = sem("lora_done"), sem("lora_ready")
        p1_done, p1_ready = sem("p1_done"), sem("p1_ready")
        x1_done, x1_ready = sem("x1_done"), sem("x1_ready")
        x2_done, x2_ready = sem("x2_done"), sem("x2_ready")
        g_done, u_done, gelu_ready, hid_ready, down_done = (
            sem("g_done"), sem("u_done"), sem("gelu_ready"), sem("hid_ready"), sem("down_done"))
        x2s_ready = sem("x2s_ready")
        w3t_done, w3t_ready = sem("w3t_done"), sem("w3t_ready")
        x3_ready, x3b_ready = sem("x3_ready"), sem("x3b_ready")
        ug3_done, tanh3_ready, sig3_ready, gsig3_ready, hid3_ready = (
            sem("ug3_done"), sem("tanh3_ready"), sem("sig3_ready"), sem("gsig3_ready"), sem("hid3_ready"))
        out_done, out_ready = sem("out_done"), sem("out_ready")

        def columns(b):
            return bass.DynSlice(b * S, S)

        def fills(b, q):
            return (b - q) // 2 + 1

        block = ctx.enter_context(nc.Block())

        @block.sync
        def _(sp):
            sp.dma_start(condb[:, :], cond.rearrange("b e -> (b e)").partition_broadcast(128)).then_inc(cond_in, 16)
            for h in range(2):
                sp.dma_start(x_in[:, HALF * h:HALF * (h + 1), :],
                             x[HALF * h:HALF * (h + 1), :, :].rearrange("b s c -> s b c")).then_inc(x_loaded[h], 16)
            sp.dma_start(w1_sb[:, :, :], w1.rearrange("g (oh ol) t -> (g oh) ol t", ol=OL)).then_inc(w1_in, 16)
            sp.dma_start(shg[:, :], sh_gate).then_inc(sh_in, 16)
            sp.dma_start(shu[:, :], sh_up).then_inc(sh_in, 16)
            sp.dma_start(shd[:, :, :], sh_down.rearrange("(p t) c -> p t c", t=T)).then_inc(shd_in, 16)
            sp.wait_ge(routed, 1)

            def load_pair(b, k, q, used=None):
                slot = TOP_K * q + k
                e = sp.value_load(chosen[0:1, bass.DynSlice(TOP_K * b + k, 1)], min_val=0, max_val=E - 1)
                if used is not None:
                    sp.wait_ge(down_done, used)
                sp.dma_start(gate_w[:, slot, :],
                             sk_gate[bass.DynSlice(e, 1), :, :].rearrange("o h i -> (o h) i")).then_inc(pair_in[slot], 16)
                sp.dma_start(up_w[:, slot, :],
                             sk_up[bass.DynSlice(e, 1), :, :].rearrange("o h i -> (o h) i")).then_inc(pair_in[slot], 16)
                sp.dma_start(down_w[:, slot, :, :],
                             sk_down[bass.DynSlice(e, 1), :, :].rearrange("o (p t) c -> (o p) t c", t=T)
                             ).then_inc(pair_in[slot], 16)

            def load_w3(b, q, used=None):
                e = sp.value_load(chosen[0:1, bass.DynSlice(TOP_K * b, 1)], min_val=0, max_val=E - 1)
                if used is not None:
                    sp.wait_ge(w3t_done, used)
                for n, w in enumerate((w_up, w_gate)):
                    sp.dma_start(w3[:, q, n, :], w[bass.DynSlice(e, 1), :, :].rearrange("o (p c) d -> (o p) (c d)", c=HC)
                                 ).then_inc(w3_in[q], 16)
                sp.dma_start(w3[:, q, 2, :], w_down[bass.DynSlice(e, 1), :, :].rearrange("o d h -> (o d) h")
                             ).then_inc(w3_in[q], 16)

            def store(b, q):
                sp.wait_ge(out_ready, b + 1)
                sp.dma_start(out[bass.DynSlice(b, 1), :, :].rearrange("o s c -> (o s) c"),
                             out_sb[:, q, :]).then_inc(stored[q], 16)

            def refill(b, q, first=True, second=True, stores=True):
                if first:
                    load_pair(b + 1, 1, 1 - q, NSH + TOP_K * b)
                if stores:
                    store(b - 2, q)
                if first:
                    load_w3(b + 1, 1 - q, 2 * b)
                if second:
                    load_pair(b + 2, 0, q, NSH + TOP_K * b + 1)

            for b in range(2):
                for k in range(TOP_K):
                    load_pair(b, k, b)
                load_w3(b, b)
            refill(0, 0, first=False, stores=False)
            refill(1, 1, stores=False)
            with sp.Fori(1, 3) as j:
                for q in range(2):
                    refill(2 * j + q, q)
            refill(B - 2, 0, second=False)
            store(B - 3, 1)
            store(B - 2, 0)
            store(B - 1, 1)
            for q in range(2):
                sp.wait_ge(stored[q], 16 * (B // 2))

        @block.gpsimd
        def _(pool):
            pool.memset(ident[:, :], 0.0).then_inc(pool_step, 1)
            pool.memset(seg[:, :], 1.0).then_inc(pool_step, 1)
            pool.wait_ge(pool_step, 2)
            pool.affine_select(out=ident[:, :], in_=ident[:, :], compare_op=ALU.not_equal, fill=1.0, base=0,
                               pattern=[[-1, 128]], channel_multiplier=1).then_inc(consts, 1)
            pool.affine_select(out=seg[:, :], in_=seg[:, :], compare_op=ALU.is_ge, fill=0.0, base=0,
                               pattern=[[-R, E]], channel_multiplier=1).then_inc(pool_step, 1)
            pool.wait_ge(pool_step, 3)
            pool.affine_select(out=seg[:, :], in_=seg[:, :], compare_op=ALU.is_ge, fill=0.0, base=R - 1,
                               pattern=[[R, E]], channel_multiplier=-1).then_inc(consts, 1)
            pool.iota(rev[:, :], [[-1, E]], base=E, channel_multiplier=0,
                      allow_small_or_imprecise_dtypes=True).then_inc(consts, 1)
            pool.iota(revp[:, :], [[0, 1]], base=E, channel_multiplier=-1,
                      allow_small_or_imprecise_dtypes=True).then_inc(consts, 1)

        @block.scalar
        def _(act):
            act.dma_start(small[:, 0, :], w_base).then_inc(small_in, 16)
            act.dma_start(small[:, 1, :], a_s.rearrange("e r c -> (e r) c")).then_inc(small_in, 16)
            act.dma_start(small[:, 2, :].rearrange("o (e r) -> o e r", r=R), b_s.rearrange("e o r -> o e r")
                          ).then_inc(small_in, 16)
            act.dma_start(small[:, 3, :], mask).then_inc(small_in, 16)
            act.dma_start(b0col[:, :], b_base.rearrange("(o a) -> o a", a=1)).then_inc(bias_in, 16)
            act.dma_start(b1col[:, :], bias1.rearrange("(o a) -> o a", a=1)).then_inc(bias_in, 16)
            act.dma_start(bias3[:, 0:H], b_up).then_inc(bias3_in, 16)
            act.dma_start(bias3[:, H:2 * H], b_gate).then_inc(bias3_in, 16)
            act.dma_start(bias3[:, 2 * H:2 * H + C], b_down).then_inc(bias3_in, 16)

            act.wait_ge(shifted_ready, 1)
            act.activation(expo[:, :, :], shifted[:, :, :], ACT.Exp).then_inc(expo_ready, 1)
            for h in range(2):
                act.wait_ge(xt_done, h + 1)
                act.activation(x_t[:, N * h:N * (h + 1)], bank[h][:, :], ACT.Copy).then_inc(xt_ready, 1)

            def gelu_step(k, n):
                act.wait_ge(g_done, k + 1)
                if not isinstance(k, int) or k >= 2:
                    act.wait_ge(hid_ready, k - 1)
                act.activation(gelu[:, n, :], g_ps[n][:, :], ACT.Gelu_apprx_tanh).then_inc(gelu_ready, 1)

            def copy_out(b, q):
                act.wait_ge(out_done, b + 1)
                if not isinstance(b, int) or b >= 2:
                    act.wait_ge(stored[q], 16 * (fills(b, q) - 1))
                act.activation(out_sb[:, q, :], out_ps[:, 0:C], ACT.Copy).then_inc(out_ready, 1)

            def copy_w3_up_gate(b):
                act.wait_ge(w3t_done, 2 * b + 1)
                act.activation(w3_t[:, 0:2, :, :].rearrange("p n c d -> p (n c d)"), w3a_ps[:, :],
                               ACT.Copy).then_inc(w3t_ready, 1)

            def copy_w3_down(b):
                act.wait_ge(w3t_done, 2 * b + 2)
                act.activation(w3_t[:, 2, :, :].rearrange("p c d -> p (c d)"), w3b_ps[:, H:2 * H],
                               ACT.Copy).then_inc(w3t_ready, 1)

            def tanh_step(b):
                act.wait_ge(ug3_done, b + 1)
                if isinstance(b, int) and b == 0:
                    act.wait_ge(bsel_ready, 2)
                if not isinstance(b, int) or b >= 1:
                    act.wait_ge(sig3_ready, b)
                for c in range(HC):
                    act.activation(tanh3[:, c, :], ug3_ps[:, S * c:S * (c + 1)], ACT.Tanh,
                                   bias=bhalf[:, c, bass.DynSlice(b, 1)], scale=0.5).then_inc(tanh3_ready, 1)

            def batch(b, q, last=True, before_last=True):
                gelu_step(NSH + TOP_K * b, 0)
                if before_last:
                    copy_out(b - 2, q)
                if last:
                    copy_w3_up_gate(b - 1)
                gelu_step(NSH + TOP_K * b + 1, 1)
                if last:
                    copy_w3_down(b - 1)
                    tanh_step(b - 1)

            for k in range(NSH):
                gelu_step(k, k % 2)
            batch(0, 0, last=False, before_last=False)
            batch(1, 1, before_last=False)
            with act.Fori(1, B // 2) as j:
                for q in range(2):
                    batch(2 * j + q, q)
            copy_out(B - 2, 0)
            copy_w3_up_gate(B - 1)
            copy_w3_down(B - 1)
            tanh_step(B - 1)
            copy_out(B - 1, 1)

        @block.vector
        def _(dve):
            steps = [0]

            def then(ins):
                steps[0] += 1
                ins.then_inc(dve_step, 1)
                dve.wait_ge(dve_step, steps[0])

            def over_e(a):
                return a.unsqueeze(2).broadcast_to([128, B, E])

            def over_b(a):
                return a.unsqueeze(1).broadcast_to([128, B, a.shape[1]])

            cond3 = condb[:, :].rearrange("p (b e) -> p b e", e=E)
            dve.wait_ge(cond_in, 16)
            dve.wait_ge(consts, 4)
            then(dve.tensor_tensor(segcond[:, :, :], cond3, over_b(seg[:, :]), ALU.mult))
            then(dve.reduce_sum(wcol[:, :], segcond[:, :, :], axis=AX.X))
            then(dve.tensor_scalar(wcol2[:, :], wcol[:, :], SCALING, None, ALU.mult))
            then(dve.reduce_sum(delta[:, :], ident[:, :].rearrange("p (e j) -> p j e", j=OH), axis=AX.X))
            dve.tensor_tensor(mix1[:, :, :], wcol[:, :].unsqueeze(2).broadcast_to([128, B, OH]),
                              over_b(delta[:, :]), ALU.mult).then_inc(mix_ready, 1)
            then(dve.reduce_max(m1[:, :], cond3, axis=AX.X))
            then(dve.tensor_tensor(eq[:, :, :], cond3, over_e(m1[:, :]), ALU.is_equal))
            then(dve.tensor_tensor(val[:, :, :], eq[:, :, :], over_b(rev[:, :]), ALU.mult))
            then(dve.reduce_max(rank[:, 0, :], val[:, :, :], axis=AX.X))
            then(dve.tensor_tensor(hot1[:, :, :], val[:, :, :], over_e(rank[:, 0, :]), ALU.is_equal))
            then(dve.scalar_tensor_tensor(rest[:, :, :], hot1[:, :, :], LOWEST, cond3, ALU.mult, ALU.add))
            then(dve.reduce_max(m2[:, :], rest[:, :, :], axis=AX.X))
            then(dve.tensor_tensor(eq[:, :, :], rest[:, :, :], over_e(m2[:, :]), ALU.is_equal))
            then(dve.tensor_tensor(val[:, :, :], eq[:, :, :], over_b(rev[:, :]), ALU.mult))
            then(dve.reduce_max(rank[:, 1, :], val[:, :, :], axis=AX.X))
            then(dve.tensor_tensor(hot2[:, :, :], val[:, :, :], over_e(rank[:, 1, :]), ALU.is_equal))
            dve.tensor_scalar(chosen[:, :].rearrange("p (b k) -> p k b", k=TOP_K), rank[:, :, :], -1.0, float(E),
                              ALU.mult, ALU.add).then_inc(routed, 1)
            dve.tensor_scalar(hot_t[:, :], rank[0:E, 0, :], revp[:, 0:1], None, ALU.is_equal).then_inc(hot_ready, 1)
            dve.tensor_tensor(shifted[:, :, :], cond3, over_e(m1[:, :]), ALU.subtract).then_inc(shifted_ready, 1)

            dve.wait_ge(smallt_done, 1)
            dve.tensor_copy(small_t[:, :, :].rearrange("p n c -> p (n c)"), bank[2][:, :]).then_inc(smallt_ready, 1)
            dve.wait_ge(bias_in, 32)
            for h in range(2):
                dve.wait_ge(lora_done, h + 1)
                dve.tensor_tensor(lora[:, N * h:N * (h + 1)].rearrange("p (b s) -> p b s", s=S),
                                  bank[3 + h][:, :].rearrange("p (b s) -> p b s", s=S),
                                  wcol2[:, HALF * h:HALF * (h + 1)].unsqueeze(2).broadcast_to([128, HALF, S]),
                                  ALU.mult).then_inc(lora_ready, 1)
            dve.wait_ge(smallt_ready, 1)
            for h in range(2):
                for a in range(OL // 2):
                    ol = h * (OL // 2) + a
                    if a == 0:
                        dve.wait_ge(p1_done, h + 1)
                    last = dve.tensor_tensor(
                        p1[:, :, ol:C:OL],
                        bank[5 + h][:, 128 * a:128 * (a + 1)].rearrange("t (b oh) -> t b oh", oh=OH),
                        mask_t[:, ol:C:OL].unsqueeze(1).broadcast_to([128, B, OH]), ALU.mult)
                last.then_inc(p1_ready, 1)
            for h in range(2):
                dve.wait_ge(x1_done, h + 1)
                dve.wait_ge(xt_ready, h + 1)
                dve.scalar_tensor_tensor(x1_t[:, N * h:N * (h + 1)], bank[h][:, :], b0col[:, 0:1],
                                         x_t[:, N * h:N * (h + 1)], ALU.add, ALU.add).then_inc(x1_ready, 1)
            for h in range(2):
                dve.wait_ge(x2_done, h + 1)
                dve.wait_ge(x1_ready, h + 1)
                dve.scalar_tensor_tensor(x2_t[:, N * h:N * (h + 1)], bank[3 + h][:, :], b1col[:, 0:1],
                                         x1_t[:, N * h:N * (h + 1)], ALU.add, ALU.add).then_inc(x2_ready, 1)

            dve.wait_ge(expo_ready, 1)
            then(dve.reduce_sum(total[:, :], expo[:, :, :], axis=AX.X))
            then(dve.reciprocal(rtotal[:, :], total[:, :]))
            then(dve.tensor_tensor(prob[:, :, :], expo[:, :, :], over_e(rtotal[:, :]), ALU.mult))
            for k, hot in enumerate((hot1, hot2)):
                then(dve.tensor_tensor(picked[:, :, :], prob[:, :, :], hot[:, :, :], ALU.mult))
                then(dve.reduce_sum(pk[:, :, k], picked[:, :, :], axis=AX.X))
            then(dve.reduce_sum(pksum[:, :], pk[:, :, :], axis=AX.X))
            then(dve.reciprocal(rpksum[:, :], pksum[:, :]))
            then(dve.tensor_tensor(wnorm[:, :, :], pk[:, :, :], rpksum[:, :].unsqueeze(2).broadcast_to([128, B, TOP_K]),
                                   ALU.mult))
            then(dve.tensor_scalar(wpart[:, :, :], wnorm[:, :, :], 1.0 - STOP_SCALE, None, ALU.mult))
            then(dve.scalar_tensor_tensor(wsel[:, :].rearrange("p (b k) -> p b k", k=TOP_K), wnorm[:, :, :], STOP_SCALE,
                                          wpart[:, :, :], ALU.mult, ALU.add))
            dve.wait_ge(bias_sel, 1)
            then(dve.tensor_copy(bsel[:, :, :].rearrange("p n b -> p (n b)"), bank[7][:, 0:(2 * HC + 1) * B]))
            dve.sem_inc(bsel_ready, 1)
            dve.tensor_scalar(bhalf[:, :, :], bsel[:, 0:HC, :], 0.5, None, ALU.mult).then_inc(bsel_ready, 1)

            def hidden(k, n, weight=None):
                dve.wait_ge(gelu_ready, k + 1)
                dve.wait_ge(u_done, k + 1)
                if not isinstance(k, int) or k >= 2:
                    dve.wait_ge(down_done, k - 1)
                if weight is None:
                    dve.tensor_tensor(hid[:, n, :], gelu[:, n, :], u_ps[n][:, :], ALU.mult).then_inc(hid_ready, 1)
                else:
                    dve.scalar_tensor_tensor(hid[:, n, :], gelu[:, n, :], wsel[:, bass.DynSlice(weight, 1)],
                                             u_ps[n][:, :], ALU.mult, ALU.mult).then_inc(hid_ready, 1)

            def add_shared(h):
                dve.wait_ge(down_done, T * (h + 1))
                dve.tensor_tensor(x2s[:, N * h:N * (h + 1)], sh_acc[h][:, :], x2_t[:, N * h:N * (h + 1)],
                                  ALU.add).then_inc(x2s_ready, 1)

            def residual(b, q):
                dve.wait_ge(down_done, NSH + TOP_K * (b + 1))
                if not isinstance(b, int) or b >= 2:
                    dve.wait_ge(out_done, b - 1)
                dve.tensor_tensor(x3_t[:, q, :], acc_ps[:, 0:S], x2s[:, columns(b)], ALU.add).then_inc(x3_ready, 1)
                dve.wait_ge(x3_ready, b + 1)
                dve.tensor_scalar(x3b_t[:, q, :], x3_t[:, q, :], bsel[:, 2 * HC, bass.DynSlice(b, 1)], None,
                                  ALU.add).then_inc(x3b_ready, 1)

            def hidden3(b):
                dve.wait_ge(tanh3_ready, HC * (b + 1))
                dve.tensor_scalar(sig3[:, :, :], tanh3[:, :, :], 0.5, 0.5, ALU.mult, ALU.add).then_inc(sig3_ready, 1)
                dve.wait_ge(sig3_ready, b + 1)
                dve.wait_ge(ug3_done, b + 1)
                for c in range(HC):
                    dve.scalar_tensor_tensor(gsig3[:, c, :], ug3_ps[:, S * (HC + c):S * (HC + c + 1)],
                                             bsel[:, HC + c, bass.DynSlice(b, 1)], sig3[:, c, :],
                                             ALU.add, ALU.mult).then_inc(gsig3_ready, 1)
                dve.wait_ge(gsig3_ready, HC * (b + 1))
                if not isinstance(b, int) or b >= 1:
                    dve.wait_ge(out_done, b)
                for c in range(HC):
                    dve.scalar_tensor_tensor(hid3[:, c, :], ug3_ps[:, S * c:S * (c + 1)],
                                             bsel[:, c, bass.DynSlice(b, 1)], gsig3[:, c, :],
                                             ALU.add, ALU.mult).then_inc(hid3_ready, 1)

            def batch(b, q, last=True):
                hidden(NSH + TOP_K * b, 0, TOP_K * b)
                if last:
                    residual(b - 1, 1 - q)
                hidden(NSH + TOP_K * b + 1, 1, TOP_K * b + 1)
                if last:
                    hidden3(b - 1)

            for k in range(NSH):
                hidden(k, k % 2)
                if k == T:
                    add_shared(0)
            batch(0, 0, last=False)
            add_shared(1)
            batch(1, 1)
            with dve.Fori(1, B // 2) as j:
                for q in range(2):
                    batch(2 * j + q, q)
            residual(B - 1, 1)
            hidden3(B - 1)

        @block.tensor
        def _(pe):
            pe.wait_ge(consts, 1)
            for h in range(2):
                pe.wait_ge(x_loaded[h], 16)
                for n in range(HALF):
                    mm = pe.transpose(bank[h][:, S * n:S * (n + 1)], x_in[:, HALF * h + n, :], ident[:, :])
                mm.then_inc(xt_done, 1)
            pe.wait_ge(small_in, 64)
            for n in range(4):
                mm = pe.transpose(bank[2][:, 128 * n:128 * (n + 1)], small[:, n, :], ident[:, :])
            mm.then_inc(smallt_done, 1)
            pe.wait_ge(smallt_ready, 1)
            for h in range(2):
                pe.wait_ge(xt_ready, h + 1)
                pe.matmul(bank[3 + h][:, :], a_t, x_t[:, N * h:N * (h + 1)], start=True, stop=True).then_inc(lora_done, 1)
            pe.wait_ge(mix_ready, 1)
            pe.wait_ge(w1_in, 16)
            for h in range(2):
                for a in range(OL // 2):
                    mm = pe.matmul(bank[5 + h][:, 128 * a:128 * (a + 1)], w1_sb[:, h * (OL // 2) + a, :],
                                   mix1[:, :, :].rearrange("p b j -> p (b j)"), start=True, stop=True)
                mm.then_inc(p1_done, 1)
            for h in range(2):
                pe.matmul(bank[h][:, :], base_t, x_t[:, N * h:N * (h + 1)], start=True, stop=False)
                pe.wait_ge(lora_ready, h + 1)
                pe.matmul(bank[h][:, :], b_t, lora[:, N * h:N * (h + 1)], start=False, stop=True).then_inc(x1_done, 1)
            pe.wait_ge(p1_ready, 2)
            for h in range(2):
                pe.wait_ge(x1_ready, h + 1)
                for n in range(HALF):
                    b = HALF * h + n
                    mm = pe.matmul(bank[3 + h][:, S * n:S * (n + 1)], p1[:, b, :], x1_t[:, columns(b)],
                                   start=True, stop=True)
                mm.then_inc(x2_done, 1)
            pe.wait_ge(bias3_in, 48)
            pe.wait_ge(hot_ready, 1)
            for n in range(2 * HC + 1):
                lhs = bias3[:, 2 * H:2 * H + C] if n == 2 * HC else \
                    bias3[:, H * (n // HC) + n % HC:H * (n // HC + 1):HC]
                mm = pe.matmul(bank[7][:, B * n:B * (n + 1)], lhs, hot_t[:, :], start=True, stop=True)
            mm.then_inc(bias_sel, 1)

            def shared_gate_up(k):
                h, t, n = k // T, k % T, k % 2
                if t == 0:
                    pe.wait_ge(x2_ready, h + 1)
                if k >= 2:
                    pe.wait_ge(hid_ready, k - 1)
                rhs = x2_t[:, N * h:N * (h + 1)]
                pe.matmul(g_ps[n][:, :], shg[:, t:I:T], rhs, start=True, stop=True).then_inc(g_done, 1)
                pe.matmul(u_ps[n][:, :], shu[:, t:I:T], rhs, start=True, stop=True).then_inc(u_done, 1)

            def shared_down(k):
                h, t, n = k // T, k % T, k % 2
                pe.wait_ge(hid_ready, k + 1)
                pe.matmul(sh_acc[h][:, :], shd[:, t, :], hid[:, n, :], start=(t == 0), stop=(t == T - 1)
                          ).then_inc(down_done, 1)

            def gate_up(b, k, q):
                slot, step = TOP_K * q + k, NSH + TOP_K * b + k
                pe.wait_ge(pair_in[slot], fills(b, q) * 48)
                pe.wait_ge(hid_ready, step - 1)
                for ps, w, done in ((g_ps[k], gate_w, g_done), (u_ps[k], up_w, u_done)):
                    for t in range(T):
                        mm = pe.matmul(ps[:, S * t:S * (t + 1)], w[:, slot, t:I:T], x2_t[:, columns(b)],
                                       start=True, stop=True)
                    mm.then_inc(done, 1)

            def down(b, k, q):
                slot, step = TOP_K * q + k, NSH + TOP_K * b + k
                pe.wait_ge(hid_ready, step + 1)
                if k == 0 and (not isinstance(b, int) or b >= 1):
                    pe.wait_ge(x3_ready, b)
                for t in range(T):
                    mm = pe.matmul(acc_ps[:, 0:S], down_w[:, slot, t, :], hid[:, k, S * t:S * (t + 1)],
                                   start=(k == 0 and t == 0), stop=(k == TOP_K - 1 and t == T - 1))
                mm.then_inc(down_done, 1)

            def turn_w3_up_gate(b, q):
                pe.wait_ge(w3_in[q], fills(b, q) * 48)
                if isinstance(b, int) and b == 0:
                    pe.wait_ge(x2s_ready, 1)
                else:
                    pe.wait_ge(w3t_ready, 2 * b - 1)
                for n in range(2):
                    for c in range(HC):
                        mm = pe.transpose(w3a_ps[:, 128 * (HC * n + c):128 * (HC * n + c + 1)],
                                          w3[:, q, n, C * c:C * (c + 1)], ident[:, :])
                mm.then_inc(w3t_done, 1)

            def turn_w3_down(b, q):
                if not isinstance(b, int) or b >= 1:
                    pe.wait_ge(out_ready, b)
                for c in range(HC):
                    mm = pe.transpose(w3b_ps[:, H + 128 * c:H + 128 * (c + 1)], w3[:, q, 2, c:H:HC], ident[:, :])
                mm.then_inc(w3t_done, 1)

            def up_gate3(b, q):
                pe.wait_ge(w3t_ready, 2 * b + 1)
                pe.wait_ge(x3_ready, b + 1)
                if isinstance(b, int) and b == 0:
                    pe.wait_ge(x2s_ready, 2)
                else:
                    pe.wait_ge(hid3_ready, HC * b)
                for n in range(2):
                    for c in range(HC):
                        mm = pe.matmul(ug3_ps[:, S * (HC * n + c):S * (HC * n + c + 1)], w3_t[:, n, c, :],
                                       x3_t[:, q, :], start=True, stop=True)
                mm.then_inc(ug3_done, 1)

            def down3(b, q):
                pe.wait_ge(x3b_ready, b + 1)
                pe.wait_ge(w3t_ready, 2 * b + 2)
                pe.matmul(out_ps[:, 0:C], x3b_t[:, q, :], ident[:, :], start=True, stop=False)
                pe.wait_ge(hid3_ready, HC * (b + 1))
                for c in range(HC):
                    mm = pe.matmul(out_ps[:, 0:C], hid3[:, c, :], w3_t[:, 2, c, :], start=False, stop=(c == HC - 1))
                mm.then_inc(out_done, 1)

            def batch(b, q, last=True, before_last=True):
                gate_up(b, 0, q)
                if last:
                    down(b - 1, 1, 1 - q)
                if before_last:
                    down3(b - 2, q)
                if last:
                    turn_w3_up_gate(b - 1, 1 - q)
                gate_up(b, 1, q)
                if last:
                    turn_w3_down(b - 1, 1 - q)
                    up_gate3(b - 1, 1 - q)
                down(b, 0, q)

            pe.wait_ge(sh_in, 32)
            pe.wait_ge(bsel_ready, 1)
            shared_gate_up(0)
            pe.wait_ge(shd_in, 16)
            for k in range(1, NSH):
                shared_gate_up(k)
                shared_down(k - 1)
            gate_up(0, 0, 0)
            shared_down(NSH - 1)
            gate_up(0, 1, 0)
            down(0, 0, 0)
            batch(1, 1, before_last=False)
            with pe.Fori(1, B // 2) as j:
                for q in range(2):
                    batch(2 * j + q, q)
            down(B - 1, 1, 1)
            down3(B - 2, 0)
            turn_w3_up_gate(B - 1, 1)
            turn_w3_down(B - 1, 1)
            up_gate3(B - 1, 1)
            down3(B - 1, 1)


_INS = ['x', 'cond_8', 'L0_cond_W_base', 'L0_cond_b_base', 'L0_cond_As', 'L0_cond_Bs', 'L1_cond_weight',
        'L1_cond_mask', 'L1_cond_bias', 'L2_cond_skill_gate', 'L2_cond_skill_up', 'L2_cond_skill_down',
        'L2_cond_shared_gate', 'L2_cond_shared_up', 'L2_cond_shared_down', 'L3_cond_W_up', 'L3_cond_b_up',
        'L3_cond_W_gate', 'L3_cond_b_gate', 'L3_cond_W_down', 'L3_cond_b_down']


def kernel(**inputs):
    import numpy as _np
    import concourse.bacc as _bacc
    from concourse import mybir as _mybir
    from concourse.bass_utils import run_bass_kernel_spmd as _run

    nc = _bacc.Bacc("TRN2", target_bir_lowering=False, num_devices=1)
    arrays, args = {}, []
    for name in _INS:
        a = _np.ascontiguousarray(inputs[name])
        arrays[f"in_{name}"] = a
        args.append(nc.dram_tensor(f"in_{name}", a.shape, _mybir.dt.from_np(a.dtype), kind="ExternalInput").ap())
    args.append(nc.dram_tensor("out_x", (B, S, C), _mybir.dt.float32, kind="ExternalOutput").ap())
    build(nc, *args)
    return _run(nc, [arrays], core_ids=[0]).results[0]["out_x"]
```

```python
import concourse.bass as bass
from concourse import mybir
from contextlib import ExitStack

B, S, C = 8, 128, 128
E = 8
R = 16
I = 512
H = 256
T = I // 128
HC = H // 128
OL = E * C // 128
OH = C // OL
HALF = B // 2
N = HALF * S
TOP_K = 2
SCALING = 32.0 / R
STOP_SCALE = 1.0 / 12
NSH = 2 * T
LOWEST = -3.0e38


def build(nc, x, cond, w_base, b_base, a_s, b_s, w1, mask, bias1, sk_gate, sk_up, sk_down,
          sh_gate, sh_up, sh_down, w_up, b_up, w_gate, b_gate, w_down, b_down, out):
    fp32, i32 = mybir.dt.float32, mybir.dt.int32
    ALU, ACT, AX = mybir.AluOpType, mybir.ActivationFunctionType, mybir.AxisListType

    ctx = ExitStack()
    with ctx:
        ctx.enter_context(nc.allow_non_contiguous_dma(reason="columns of biases"))

        def sb(name, shape, dt=fp32):
            return ctx.enter_context(nc.sbuf_tensor(name, shape, dt))

        def sem(name):
            return ctx.enter_context(nc.semaphore(name))

        ident = sb("ident", [128, 128])
        seg = sb("seg", [128, E])
        delta = sb("delta", [128, OH])
        rev = sb("rev", [128, E])
        revp = sb("revp", [E, 1])
        condb = sb("condb", [128, B * E])
        segcond = sb("segcond", [128, B, E])
        wcol = sb("wcol", [128, B])
        wcol2 = sb("wcol2", [128, B])
        mix1 = sb("mix1", [128, B, OH])
        m1 = sb("m1", [128, B])
        m2 = sb("m2", [128, B])
        eq = sb("eq", [128, B, E])
        val = sb("val", [128, B, E])
        rank = sb("rank", [128, TOP_K, B])
        hot1 = sb("hot1", [128, B, E])
        hot2 = sb("hot2", [128, B, E])
        rest = sb("rest", [128, B, E])
        chosen = sb("chosen", [128, B * TOP_K], i32)
        shifted = sb("shifted", [128, B, E])
        expo = sb("expo", [128, B, E])
        total = sb("total", [128, B])
        rtotal = sb("rtotal", [128, B])
        prob = sb("prob", [128, B, E])
        picked = sb("picked", [128, B, E])
        pk = sb("pk", [128, B, TOP_K])
        pksum = sb("pksum", [128, B])
        rpksum = sb("rpksum", [128, B])
        wnorm = sb("wnorm", [128, B, TOP_K])
        wpart = sb("wpart", [128, B, TOP_K])
        wsel = sb("wsel", [128, B * TOP_K])
        hot_t = sb("hot_t", [E, B])

        x_in = sb("x_in", [S, B, C])
        a_sb = sb("a_sb", [128, C])
        b_sb = sb("b_sb", [C, 128])
        base_sb = sb("base_sb", [C, C])
        mask_sb = sb("mask_sb", [C, C])
        small_t = sb("small_t", [C, 2, C])
        base_t, mask_t = small_t[:, 0, :], small_t[:, 1, :]
        warm = sb("warm", [128, 128])
        b0col = sb("b0col", [C, 1])
        b1col = sb("b1col", [C, 1])
        w1_sb = sb("w1_sb", [128, OL, C])
        p1 = sb("p1", [C, B, C])
        b_mix = sb("b_mix", [128, B, C])
        p0 = sb("p0", [C, B, C])
        x_t = sb("x_t", [C, B * S])
        x1_t = sb("x1_t", [C, B * S])
        x2_t = sb("x2_t", [C, B * S])
        x2s = sb("x2s", [C, B * S])
        shg = sb("shg", [128, I])
        shu = sb("shu", [128, I])
        shd = sb("shd", [128, T, C])
        gate_w = sb("gate_w", [128, 2 * TOP_K, I])
        up_w = sb("up_w", [128, 2 * TOP_K, I])
        down_w = sb("down_w", [128, 2 * TOP_K, T, C])
        gelu = sb("gelu", [128, 2, N])
        hid = sb("hid", [128, 2, N])
        w3 = sb("w3", [128, 2, 3, H])
        w3_t = sb("w3_t", [128, 3, HC, 128])
        bias3 = sb("bias3", [E, 2 * H + C])
        bsel = sb("bsel", [128, 2 * HC + 1, B])
        x3_t = sb("x3_t", [C, 2, S])
        x3b_t = sb("x3b_t", [C, 2, S])
        half3 = sb("half3", [128, HC, S])
        tanh3 = sb("tanh3", [128, HC, S])
        gate3 = sb("gate3", [128, HC, S])
        hid3 = sb("hid3", [128, HC, S])
        out_sb = sb("out_sb", [S, 2, C])

        bank = [ctx.enter_context(nc.psum_tensor(f"bank{n}", [128, 512], fp32)) for n in range(8)]
        g_ps, u_ps = bank[0:2], bank[2:4]
        acc_ps = bank[4]
        sh_acc = [bank[5], bank[7]]
        w3a_ps, w3b_ps = bank[5], bank[6]
        out_ps = bank[6]
        ug3_ps = bank[7]

        cond_in, a_in, b_in, base_in, mask_in = sem("cond_in"), sem("a_in"), sem("b_in"), sem("base_in"), sem("mask_in")
        bias_in, bias3_in = sem("bias_in"), sem("bias3_in")
        x_loaded = [sem("x_loaded0"), sem("x_loaded1")]
        w1_in, sh_in, shd_in = sem("w1_in"), sem("sh_in"), sem("shd_in")
        pair_in = [sem(f"pair_in{n}") for n in range(2 * TOP_K)]
        w3_in = [sem(f"w3_in{n}") for n in range(2)]
        stored = [sem(f"stored{n}") for n in range(2)]
        pool_step = sem("pool_step")
        consts = sem("consts")
        dve_step = sem("dve_step")
        mix_ready, routed, shifted_ready, expo_ready = sem("mix_ready"), sem("routed"), sem("shifted_ready"), sem("expo_ready")
        warm_ready, wcol_ready = sem("warm_ready"), sem("wcol_ready")
        hot_ready, bias_sel, bsel_ready = sem("hot_ready"), sem("bias_sel"), sem("bsel_ready")
        xt_done, xt_ready = sem("xt_done"), sem("xt_ready")
        bt_done, smallt_done, smallt_ready = sem("bt_done"), sem("smallt_done"), sem("smallt_ready")
        b_mixed, p0_done, p0_ready = sem("b_mixed"), sem("p0_done"), sem("p0_ready")
        p1_done, p1_ready = sem("p1_done"), sem("p1_ready")
        x1_done, x1_ready = sem("x1_done"), sem("x1_ready")
        x2_done, x2_ready = sem("x2_done"), sem("x2_ready")
        g_done, u_done, gelu_ready, hid_ready, down_done = (
            sem("g_done"), sem("u_done"), sem("gelu_ready"), sem("hid_ready"), sem("down_done"))
        x2s_ready = sem("x2s_ready")
        w3t_done, w3t_ready = sem("w3t_done"), sem("w3t_ready")
        x3_ready, x3b_ready = sem("x3_ready"), sem("x3b_ready")
        ug3_done, half3_ready, tanh3_ready, gate3_ready, hid3_ready = (
            sem("ug3_done"), sem("half3_ready"), sem("tanh3_ready"), sem("gate3_ready"), sem("hid3_ready"))
        out_done, out_ready = sem("out_done"), sem("out_ready")

        def columns(b):
            return bass.DynSlice(b * S, S)

        def fills(b, q):
            return (b - q) // 2 + 1

        block = ctx.enter_context(nc.Block())

        @block.sync
        def _(sp):
            sp.dma_start(condb[:, :], cond.rearrange("b e -> (b e)").partition_broadcast(128)).then_inc(cond_in, 16)
            for h in range(2):
                sp.dma_start(x_in[:, HALF * h:HALF * (h + 1), :],
                             x[HALF * h:HALF * (h + 1), :, :].rearrange("b s c -> s b c")).then_inc(x_loaded[h], 16)
            sp.dma_start(w1_sb[:, :, :], w1.rearrange("g (oh ol) t -> (g oh) ol t", ol=OL)).then_inc(w1_in, 16)
            sp.dma_start(shg[:, :], sh_gate).then_inc(sh_in, 16)
            sp.dma_start(shu[:, :], sh_up).then_inc(sh_in, 16)
            sp.dma_start(shd[:, :, :], sh_down.rearrange("(p t) c -> p t c", t=T)).then_inc(shd_in, 16)
            sp.wait_ge(routed, 1)

            def load_pair(b, k, q, used=None):
                slot = TOP_K * q + k
                e = sp.value_load(chosen[0:1, bass.DynSlice(TOP_K * b + k, 1)], min_val=0, max_val=E - 1)
                if used is not None:
                    sp.wait_ge(down_done, used)
                sp.dma_start(gate_w[:, slot, :],
                             sk_gate[bass.DynSlice(e, 1), :, :].rearrange("o h i -> (o h) i")).then_inc(pair_in[slot], 16)
                sp.dma_start(up_w[:, slot, :],
                             sk_up[bass.DynSlice(e, 1), :, :].rearrange("o h i -> (o h) i")).then_inc(pair_in[slot], 16)
                sp.dma_start(down_w[:, slot, :, :],
                             sk_down[bass.DynSlice(e, 1), :, :].rearrange("o (p t) c -> (o p) t c", t=T)
                             ).then_inc(pair_in[slot], 16)

            def load_w3(b, q, used=None):
                e = sp.value_load(chosen[0:1, bass.DynSlice(TOP_K * b, 1)], min_val=0, max_val=E - 1)
                if used is not None:
                    sp.wait_ge(w3t_done, used)
                for n, w in enumerate((w_up, w_gate)):
                    sp.dma_start(w3[:, q, n, :], w[bass.DynSlice(e, 1), :, :].rearrange("o (p c) d -> (o p) (c d)", c=HC)
                                 ).then_inc(w3_in[q], 16)
                sp.dma_start(w3[:, q, 2, :], w_down[bass.DynSlice(e, 1), :, :].rearrange("o d h -> (o d) h")
                             ).then_inc(w3_in[q], 16)

            def store(b, q):
                sp.wait_ge(out_ready, b + 1)
                sp.dma_start(out[bass.DynSlice(b, 1), :, :].rearrange("o s c -> (o s) c"),
                             out_sb[:, q, :]).then_inc(stored[q], 16)

            def refill(b, q, first=True, second=True, stores=True):
                if first:
                    load_pair(b + 1, 1, 1 - q, NSH + TOP_K * b)
                if stores:
                    store(b - 2, q)
                if first:
                    load_w3(b + 1, 1 - q, 2 * b)
                if second:
                    load_pair(b + 2, 0, q, NSH + TOP_K * b + 1)

            for b in range(2):
                for k in range(TOP_K):
                    load_pair(b, k, b)
                load_w3(b, b)
            refill(0, 0, first=False, stores=False)
            refill(1, 1, stores=False)
            with sp.Fori(1, 3) as j:
                for q in range(2):
                    refill(2 * j + q, q)
            refill(B - 2, 0, second=False)
            store(B - 3, 1)
            store(B - 2, 0)
            store(B - 1, 1)
            for q in range(2):
                sp.wait_ge(stored[q], 16 * (B // 2))

        @block.gpsimd
        def _(pool):
            pool.memset(ident[:, :], 0.0).then_inc(pool_step, 1)
            pool.memset(seg[:, :], 1.0).then_inc(pool_step, 1)
            pool.wait_ge(pool_step, 2)
            pool.affine_select(out=ident[:, :], in_=ident[:, :], compare_op=ALU.not_equal, fill=1.0, base=0,
                               pattern=[[-1, 128]], channel_multiplier=1).then_inc(consts, 1)
            pool.affine_select(out=seg[:, :], in_=seg[:, :], compare_op=ALU.is_ge, fill=0.0, base=0,
                               pattern=[[-R, E]], channel_multiplier=1).then_inc(pool_step, 1)
            pool.wait_ge(pool_step, 3)
            pool.affine_select(out=seg[:, :], in_=seg[:, :], compare_op=ALU.is_ge, fill=0.0, base=R - 1,
                               pattern=[[R, E]], channel_multiplier=-1).then_inc(consts, 1)
            pool.iota(rev[:, :], [[-1, E]], base=E, channel_multiplier=0,
                      allow_small_or_imprecise_dtypes=True).then_inc(consts, 1)
            pool.iota(revp[:, :], [[0, 1]], base=E, channel_multiplier=-1,
                      allow_small_or_imprecise_dtypes=True).then_inc(consts, 1)
            pool.dma_start(b0col[:, :], b_base.rearrange("(o a) -> o a", a=1)).then_inc(bias_in, 16)
            pool.dma_start(b1col[:, :], bias1.rearrange("(o a) -> o a", a=1)).then_inc(bias_in, 16)
            pool.dma_start(bias3[:, 0:H], b_up).then_inc(bias3_in, 16)
            pool.dma_start(bias3[:, H:2 * H], b_gate).then_inc(bias3_in, 16)
            pool.dma_start(bias3[:, 2 * H:2 * H + C], b_down).then_inc(bias3_in, 16)

        @block.scalar
        def _(act):
            act.dma_start(b_sb[:, :].rearrange("o (e r) -> o e r", r=R), b_s.rearrange("e o r -> o e r")
                          ).then_inc(b_in, 16)
            act.dma_start(a_sb[:, :], a_s.rearrange("e r c -> (e r) c")).then_inc(a_in, 16)
            act.dma_start(base_sb[:, :], w_base).then_inc(base_in, 16)
            act.dma_start(mask_sb[:, :], mask).then_inc(mask_in, 16)
            for h in range(2):
                act.wait_ge(xt_done, h + 1)
                act.activation(x_t[:, N * h:N * (h + 1)], bank[h][:, :], ACT.Copy).then_inc(xt_ready, 1)
            act.wait_ge(smallt_done, 1)
            act.activation(small_t[:, :, :].rearrange("p n c -> p (n c)"), bank[7][:, 0:2 * C],
                           ACT.Copy).then_inc(smallt_ready, 1)

            def gelu_step(k, n):
                act.wait_ge(g_done, k + 1)
                if not isinstance(k, int) or k >= 2:
                    act.wait_ge(hid_ready, k - 1)
                act.activation(gelu[:, n, :], g_ps[n][:, :], ACT.Gelu_apprx_tanh).then_inc(gelu_ready, 1)

            def copy_out(b, q):
                act.wait_ge(out_done, b + 1)
                if not isinstance(b, int) or b >= 2:
                    act.wait_ge(stored[q], 16 * (fills(b, q) - 1))
                act.activation(out_sb[:, q, :], out_ps[:, 0:C], ACT.Copy).then_inc(out_ready, 1)

            def copy_w3_up_gate(b):
                act.wait_ge(w3t_done, 2 * b + 1)
                act.activation(w3_t[:, 0:2, :, :].rearrange("p n c d -> p (n c d)"), w3a_ps[:, :],
                               ACT.Copy).then_inc(w3t_ready, 1)

            def copy_w3_down(b):
                act.wait_ge(w3t_done, 2 * b + 2)
                act.activation(w3_t[:, 2, :, :].rearrange("p c d -> p (c d)"), w3b_ps[:, H:2 * H],
                               ACT.Copy).then_inc(w3t_ready, 1)

            def tanh_step(b):
                act.wait_ge(half3_ready, HC * (b + 1))
                act.activation(tanh3[:, :, :], half3[:, :, :], ACT.Tanh).then_inc(tanh3_ready, 1)

            def batch(b, q, last=True, before_last=True):
                gelu_step(NSH + TOP_K * b, 0)
                if before_last:
                    copy_out(b - 2, q)
                if last:
                    copy_w3_up_gate(b - 1)
                gelu_step(NSH + TOP_K * b + 1, 1)
                if last:
                    copy_w3_down(b - 1)
                    tanh_step(b - 1)

            for k in range(NSH):
                gelu_step(k, k % 2)
                if k == 3:
                    act.wait_ge(shifted_ready, 1)
                    act.activation(expo[:, :, :], shifted[:, :, :], ACT.Exp).then_inc(expo_ready, 1)
            batch(0, 0, last=False, before_last=False)
            batch(1, 1, before_last=False)
            with act.Fori(1, B // 2) as j:
                for q in range(2):
                    batch(2 * j + q, q)
            copy_w3_up_gate(B - 1)
            copy_out(B - 2, 0)
            copy_w3_down(B - 1)
            tanh_step(B - 1)
            copy_out(B - 1, 1)

        @block.vector
        def _(dve):
            steps = [0]

            def then(ins):
                steps[0] += 1
                ins.then_inc(dve_step, 1)
                dve.wait_ge(dve_step, steps[0])

            def over_e(a):
                return a.unsqueeze(2).broadcast_to([128, B, E])

            def over_b(a):
                return a.unsqueeze(1).broadcast_to([128, B, a.shape[1]])

            dve.memset(warm[:, :], 0.0).then_inc(warm_ready, 1)
            cond3 = condb[:, :].rearrange("p (b e) -> p b e", e=E)
            dve.wait_ge(cond_in, 16)
            dve.wait_ge(consts, 4)
            then(dve.tensor_tensor(segcond[:, :, :], cond3, over_b(seg[:, :]), ALU.mult))
            then(dve.reduce_sum(wcol[:, :], segcond[:, :, :], axis=AX.X))
            then(dve.tensor_scalar(wcol2[:, :], wcol[:, :], SCALING, None, ALU.mult))
            then(dve.reduce_sum(delta[:, :], ident[:, :].rearrange("p (e j) -> p j e", j=OH), axis=AX.X))
            dve.tensor_tensor(mix1[:, :, :], wcol[:, :].unsqueeze(2).broadcast_to([128, B, OH]),
                              over_b(delta[:, :]), ALU.mult).then_inc(mix_ready, 1)
            dve.wait_ge(bt_done, 1)
            for h in range(2):
                bs = slice(HALF * h, HALF * (h + 1))
                dve.tensor_tensor(b_mix[:, bs, :], bank[2][:, 0:C].unsqueeze(1).broadcast_to([128, HALF, C]),
                                  wcol2[:, bs].unsqueeze(2).broadcast_to([128, HALF, C]), ALU.mult).then_inc(b_mixed, 1)
            dve.wait_ge(smallt_ready, 1)
            for h in range(2):
                dve.wait_ge(p0_done, h + 1)
                dve.tensor_tensor(p0[:, HALF * h:HALF * (h + 1), :], bank[3 + h][:, :].rearrange("c (b o) -> c b o", o=C),
                                  base_t.unsqueeze(1).broadcast_to([C, HALF, C]), ALU.add).then_inc(p0_ready, 1)
            for h in range(2):
                dve.wait_ge(p1_done, h + 1)
                for a in range(OL // 2):
                    ol = h * (OL // 2) + a
                    last = dve.tensor_tensor(
                        p1[:, :, ol:C:OL],
                        bank[5 + h][:, 128 * a:128 * (a + 1)].rearrange("t (b oh) -> t b oh", oh=OH),
                        mask_t[:, ol:C:OL].unsqueeze(1).broadcast_to([128, B, OH]), ALU.mult)
                last.then_inc(p1_ready, 1)
            dve.wait_ge(bias_in, 32)
            for h in range(2):
                dve.wait_ge(x1_done, h + 1)
                dve.wait_ge(xt_ready, h + 1)
                dve.scalar_tensor_tensor(x1_t[:, N * h:N * (h + 1)], bank[h][:, :], b0col[:, 0:1],
                                         x_t[:, N * h:N * (h + 1)], ALU.add, ALU.add).then_inc(x1_ready, 1)
            for h in range(2):
                dve.wait_ge(x2_done, h + 1)
                dve.wait_ge(x1_ready, h + 1)
                dve.scalar_tensor_tensor(x2_t[:, N * h:N * (h + 1)], bank[3 + h][:, :], b1col[:, 0:1],
                                         x1_t[:, N * h:N * (h + 1)], ALU.add, ALU.add).then_inc(x2_ready, 1)

            def route_first():
                then(dve.reduce_max(m1[:, :], cond3, axis=AX.X))
                then(dve.tensor_tensor(eq[:, :, :], cond3, over_e(m1[:, :]), ALU.is_equal))
                then(dve.tensor_tensor(val[:, :, :], eq[:, :, :], over_b(rev[:, :]), ALU.mult))
                then(dve.reduce_max(rank[:, 0, :], val[:, :, :], axis=AX.X))
                then(dve.tensor_tensor(hot1[:, :, :], val[:, :, :], over_e(rank[:, 0, :]), ALU.is_equal))

            def route_second():
                then(dve.scalar_tensor_tensor(rest[:, :, :], hot1[:, :, :], LOWEST, cond3, ALU.mult, ALU.add))
                then(dve.reduce_max(m2[:, :], rest[:, :, :], axis=AX.X))
                then(dve.tensor_tensor(eq[:, :, :], rest[:, :, :], over_e(m2[:, :]), ALU.is_equal))
                then(dve.tensor_tensor(val[:, :, :], eq[:, :, :], over_b(rev[:, :]), ALU.mult))
                then(dve.reduce_max(rank[:, 1, :], val[:, :, :], axis=AX.X))
                dve.tensor_scalar(chosen[:, :].rearrange("p (b k) -> p k b", k=TOP_K), rank[:, :, :], -1.0, float(E),
                                  ALU.mult, ALU.add).then_inc(routed, 1)

            def route_columns():
                then(dve.tensor_tensor(hot2[:, :, :], val[:, :, :], over_e(rank[:, 1, :]), ALU.is_equal))
                dve.tensor_scalar(hot_t[:, :], rank[0:E, 0, :], revp[:, 0:1], None, ALU.is_equal).then_inc(hot_ready, 1)
                dve.tensor_tensor(shifted[:, :, :], cond3, over_e(m1[:, :]), ALU.subtract).then_inc(shifted_ready, 1)

            def softmax():
                dve.wait_ge(expo_ready, 1)
                then(dve.reduce_sum(total[:, :], expo[:, :, :], axis=AX.X))
                then(dve.reciprocal(rtotal[:, :], total[:, :]))
                then(dve.tensor_tensor(prob[:, :, :], expo[:, :, :], over_e(rtotal[:, :]), ALU.mult))
                for k, hot in enumerate((hot1, hot2)):
                    then(dve.tensor_tensor(picked[:, :, :], prob[:, :, :], hot[:, :, :], ALU.mult))
                    then(dve.reduce_sum(pk[:, :, k], picked[:, :, :], axis=AX.X))

            def expert_weights():
                then(dve.reduce_sum(pksum[:, :], pk[:, :, :], axis=AX.X))
                then(dve.reciprocal(rpksum[:, :], pksum[:, :]))
                then(dve.tensor_tensor(wnorm[:, :, :], pk[:, :, :],
                                       rpksum[:, :].unsqueeze(2).broadcast_to([128, B, TOP_K]), ALU.mult))
                then(dve.tensor_scalar(wpart[:, :, :], wnorm[:, :, :], 1.0 - STOP_SCALE, None, ALU.mult))
                then(dve.scalar_tensor_tensor(wsel[:, :].rearrange("p (b k) -> p b k", k=TOP_K), wnorm[:, :, :],
                                              STOP_SCALE, wpart[:, :, :], ALU.mult, ALU.add))

            def bias_columns():
                dve.wait_ge(bias_sel, 1)
                dve.tensor_copy(bsel[:, :, :].rearrange("p n b -> p (n b)"), bank[6][:, 0:(2 * HC + 1) * B]
                                ).then_inc(bsel_ready, 1)
                dve.wait_ge(bsel_ready, 1)

            def hidden(k, n, weight=None):
                dve.wait_ge(gelu_ready, k + 1)
                dve.wait_ge(u_done, k + 1)
                if not isinstance(k, int) or k >= 2:
                    dve.wait_ge(down_done, k - 1)
                if weight is None:
                    dve.tensor_tensor(hid[:, n, :], gelu[:, n, :], u_ps[n][:, :], ALU.mult).then_inc(hid_ready, 1)
                else:
                    dve.scalar_tensor_tensor(hid[:, n, :], gelu[:, n, :], wsel[:, bass.DynSlice(weight, 1)],
                                             u_ps[n][:, :], ALU.mult, ALU.mult).then_inc(hid_ready, 1)

            def add_shared(h):
                dve.wait_ge(down_done, T * (h + 1))
                dve.tensor_tensor(x2s[:, N * h:N * (h + 1)], sh_acc[h][:, :], x2_t[:, N * h:N * (h + 1)],
                                  ALU.add).then_inc(x2s_ready, 1)

            def residual(b, q):
                dve.wait_ge(down_done, NSH + TOP_K * (b + 1))
                if not isinstance(b, int) or b >= 2:
                    dve.wait_ge(out_done, b - 1)
                dve.tensor_tensor(x3_t[:, q, :], acc_ps[:, 0:S], x2s[:, columns(b)], ALU.add).then_inc(x3_ready, 1)
                dve.wait_ge(x3_ready, b + 1)
                dve.tensor_scalar(x3b_t[:, q, :], x3_t[:, q, :], bsel[:, 2 * HC, bass.DynSlice(b, 1)], None,
                                  ALU.add).then_inc(x3b_ready, 1)

            def hidden3(b):
                dve.wait_ge(ug3_done, b + 1)
                if not isinstance(b, int) or b >= 1:
                    dve.wait_ge(out_done, b)
                for c in range(HC):
                    dve.tensor_scalar(half3[:, c, :], ug3_ps[:, S * c:S * (c + 1)], bsel[:, c, bass.DynSlice(b, 1)], 0.5,
                                      ALU.add, ALU.mult).then_inc(half3_ready, 1)
                dve.wait_ge(half3_ready, HC * (b + 1))
                for c in range(HC):
                    dve.scalar_tensor_tensor(gate3[:, c, :], ug3_ps[:, S * (HC + c):S * (HC + c + 1)],
                                             bsel[:, HC + c, bass.DynSlice(b, 1)], half3[:, c, :],
                                             ALU.add, ALU.mult).then_inc(gate3_ready, 1)
                dve.wait_ge(gate3_ready, HC * (b + 1))
                dve.wait_ge(tanh3_ready, b + 1)
                dve.scalar_tensor_tensor(hid3[:, :, :], tanh3[:, :, :], 1.0, gate3[:, :, :],
                                         ALU.add, ALU.mult).then_inc(hid3_ready, 1)

            def batch(b, q, last=True):
                hidden(NSH + TOP_K * b, 0, TOP_K * b)
                if last:
                    residual(b - 1, 1 - q)
                hidden(NSH + TOP_K * b + 1, 1, TOP_K * b + 1)
                if last:
                    hidden3(b - 1)

            between = [route_first, route_second, route_columns, softmax, lambda: add_shared(0), expert_weights,
                       bias_columns]
            for k in range(NSH):
                hidden(k, k % 2)
                if k < len(between):
                    between[k]()
            batch(0, 0, last=False)
            add_shared(1)
            batch(1, 1)
            with dve.Fori(1, B // 2) as j:
                for q in range(2):
                    batch(2 * j + q, q)
            residual(B - 1, 1)
            hidden3(B - 1)

        @block.tensor
        def _(pe):
            pe.wait_ge(warm_ready, 1)
            for _ in range(14):
                pe.matmul(bank[6][:, 0:128], warm[:, :], warm[:, :], start=True, stop=True)
            pe.wait_ge(consts, 1)
            pe.wait_ge(b_in, 16)
            pe.transpose(bank[2][:, 0:128], b_sb[:, :], ident[:, :]).then_inc(bt_done, 1)
            for h in range(2):
                pe.wait_ge(x_loaded[h], 16)
                for n in range(HALF):
                    mm = pe.transpose(bank[h][:, S * n:S * (n + 1)], x_in[:, HALF * h + n, :], ident[:, :])
                mm.then_inc(xt_done, 1)
            pe.wait_ge(base_in, 16)
            pe.transpose(bank[7][:, 0:C], base_sb[:, :], ident[:, :])
            pe.wait_ge(mask_in, 16)
            pe.transpose(bank[7][:, C:2 * C], mask_sb[:, :], ident[:, :]).then_inc(smallt_done, 1)
            pe.wait_ge(a_in, 16)
            for h in range(2):
                pe.wait_ge(b_mixed, h + 1)
                pe.matmul(bank[3 + h][:, :], a_sb[:, :], b_mix[:, HALF * h:HALF * (h + 1), :].rearrange("p b o -> p (b o)"),
                          start=True, stop=True).then_inc(p0_done, 1)
            pe.wait_ge(mix_ready, 1)
            pe.wait_ge(w1_in, 16)
            for h in range(2):
                for a in range(OL // 2):
                    mm = pe.matmul(bank[5 + h][:, 128 * a:128 * (a + 1)], w1_sb[:, h * (OL // 2) + a, :],
                                   mix1[:, :, :].rearrange("p b j -> p (b j)"), start=True, stop=True)
                mm.then_inc(p1_done, 1)
            for h in range(2):
                pe.wait_ge(p0_ready, h + 1)
                pe.wait_ge(xt_ready, h + 1)
                for n in range(HALF):
                    b = HALF * h + n
                    mm = pe.matmul(bank[h][:, S * n:S * (n + 1)], p0[:, b, :], x_t[:, columns(b)], start=True, stop=True)
                mm.then_inc(x1_done, 1)
            pe.wait_ge(p1_ready, 2)
            for h in range(2):
                pe.wait_ge(x1_ready, h + 1)
                for n in range(HALF):
                    b = HALF * h + n
                    mm = pe.matmul(bank[3 + h][:, S * n:S * (n + 1)], p1[:, b, :], x1_t[:, columns(b)],
                                   start=True, stop=True)
                mm.then_inc(x2_done, 1)

            def select_biases():
                pe.wait_ge(bias3_in, 48)
                pe.wait_ge(hot_ready, 1)
                for n in range(2 * HC + 1):
                    lhs = bias3[:, 2 * H:2 * H + C] if n == 2 * HC else \
                        bias3[:, H * (n // HC) + n % HC:H * (n // HC + 1):HC]
                    mm = pe.matmul(bank[6][:, B * n:B * (n + 1)], lhs, hot_t[:, :], start=True, stop=True)
                mm.then_inc(bias_sel, 1)

            def shared_gate_up(k):
                h, t, n = k // T, k % T, k % 2
                if t == 0:
                    pe.wait_ge(x2_ready, h + 1)
                if k >= 2:
                    pe.wait_ge(hid_ready, k - 1)
                rhs = x2_t[:, N * h:N * (h + 1)]
                pe.matmul(g_ps[n][:, :], shg[:, t:I:T], rhs, start=True, stop=True).then_inc(g_done, 1)
                pe.matmul(u_ps[n][:, :], shu[:, t:I:T], rhs, start=True, stop=True).then_inc(u_done, 1)

            def shared_down(k):
                h, t, n = k // T, k % T, k % 2
                pe.wait_ge(hid_ready, k + 1)
                pe.matmul(sh_acc[h][:, :], shd[:, t, :], hid[:, n, :], start=(t == 0), stop=(t == T - 1)
                          ).then_inc(down_done, 1)

            def gate_up(b, k, q):
                slot, step = TOP_K * q + k, NSH + TOP_K * b + k
                pe.wait_ge(pair_in[slot], fills(b, q) * 48)
                pe.wait_ge(hid_ready, step - 1)
                for ps, w, done in ((g_ps[k], gate_w, g_done), (u_ps[k], up_w, u_done)):
                    for t in range(T):
                        mm = pe.matmul(ps[:, S * t:S * (t + 1)], w[:, slot, t:I:T], x2_t[:, columns(b)],
                                       start=True, stop=True)
                    mm.then_inc(done, 1)

            def down(b, k, q):
                slot, step = TOP_K * q + k, NSH + TOP_K * b + k
                pe.wait_ge(hid_ready, step + 1)
                if k == 0 and (not isinstance(b, int) or b >= 1):
                    pe.wait_ge(x3_ready, b)
                for t in range(T):
                    mm = pe.matmul(acc_ps[:, 0:S], down_w[:, slot, t, :], hid[:, k, S * t:S * (t + 1)],
                                   start=(k == 0 and t == 0), stop=(k == TOP_K - 1 and t == T - 1))
                mm.then_inc(down_done, 1)

            def turn_w3_up_gate(b, q):
                pe.wait_ge(w3_in[q], fills(b, q) * 48)
                if isinstance(b, int) and b == 0:
                    pe.wait_ge(x2s_ready, 1)
                else:
                    pe.wait_ge(w3t_ready, 2 * b - 1)
                for n in range(2):
                    for c in range(HC):
                        mm = pe.transpose(w3a_ps[:, 128 * (HC * n + c):128 * (HC * n + c + 1)],
                                          w3[:, q, n, C * c:C * (c + 1)], ident[:, :])
                mm.then_inc(w3t_done, 1)

            def turn_w3_down(b, q):
                if not isinstance(b, int) or b >= 1:
                    pe.wait_ge(out_ready, b)
                for c in range(HC):
                    mm = pe.transpose(w3b_ps[:, H + 128 * c:H + 128 * (c + 1)], w3[:, q, 2, c:H:HC], ident[:, :])
                mm.then_inc(w3t_done, 1)

            def up_gate3(b, q):
                pe.wait_ge(w3t_ready, 2 * b + 1)
                pe.wait_ge(x3_ready, b + 1)
                if isinstance(b, int) and b == 0:
                    pe.wait_ge(x2s_ready, 2)
                else:
                    pe.wait_ge(gate3_ready, HC * b)
                for n in range(2):
                    for c in range(HC):
                        mm = pe.matmul(ug3_ps[:, S * (HC * n + c):S * (HC * n + c + 1)], w3_t[:, n, c, :],
                                       x3_t[:, q, :], start=True, stop=True)
                mm.then_inc(ug3_done, 1)

            def down3(b, q):
                pe.wait_ge(x3b_ready, b + 1)
                pe.wait_ge(w3t_ready, 2 * b + 2)
                pe.matmul(out_ps[:, 0:C], x3b_t[:, q, :], ident[:, :], is_transpose=True, start=True, stop=False)
                pe.wait_ge(hid3_ready, b + 1)
                for c in range(HC):
                    mm = pe.matmul(out_ps[:, 0:C], hid3[:, c, :], w3_t[:, 2, c, :], start=False, stop=(c == HC - 1))
                mm.then_inc(out_done, 1)

            def batch(b, q, last=True, before_last=True):
                gate_up(b, 0, q)
                if last:
                    down(b - 1, 1, 1 - q)
                if before_last:
                    down3(b - 2, q)
                if last:
                    turn_w3_up_gate(b - 1, 1 - q)
                gate_up(b, 1, q)
                if last:
                    turn_w3_down(b - 1, 1 - q)
                    up_gate3(b - 1, 1 - q)
                down(b, 0, q)

            pe.wait_ge(sh_in, 32)
            shared_gate_up(0)
            pe.wait_ge(shd_in, 16)
            for k in range(1, NSH):
                shared_gate_up(k)
                shared_down(k - 1)
                if k == T + 1:
                    select_biases()
            gate_up(0, 0, 0)
            shared_down(NSH - 1)
            gate_up(0, 1, 0)
            down(0, 0, 0)
            batch(1, 1, before_last=False)
            with pe.Fori(1, B // 2) as j:
                for q in range(2):
                    batch(2 * j + q, q)
            turn_w3_up_gate(B - 1, 1)
            down(B - 1, 1, 1)
            down3(B - 2, 0)
            up_gate3(B - 1, 1)
            turn_w3_down(B - 1, 1)
            down3(B - 1, 1)


_INS = ['x', 'cond_8', 'L0_cond_W_base', 'L0_cond_b_base', 'L0_cond_As', 'L0_cond_Bs', 'L1_cond_weight',
        'L1_cond_mask', 'L1_cond_bias', 'L2_cond_skill_gate', 'L2_cond_skill_up', 'L2_cond_skill_down',
        'L2_cond_shared_gate', 'L2_cond_shared_up', 'L2_cond_shared_down', 'L3_cond_W_up', 'L3_cond_b_up',
        'L3_cond_W_gate', 'L3_cond_b_gate', 'L3_cond_W_down', 'L3_cond_b_down']


def kernel(**inputs):
    import numpy as _np
    import concourse.bacc as _bacc
    from concourse import mybir as _mybir
    from concourse.bass_utils import run_bass_kernel_spmd as _run

    nc = _bacc.Bacc("TRN2", target_bir_lowering=False, num_devices=1)
    arrays, args = {}, []
    for name in _INS:
        a = _np.ascontiguousarray(inputs[name])
        arrays[f"in_{name}"] = a
        args.append(nc.dram_tensor(f"in_{name}", a.shape, _mybir.dt.from_np(a.dtype), kind="ExternalInput").ap())
    args.append(nc.dram_tensor("out_x", (B, S, C), _mybir.dt.float32, kind="ExternalOutput").ap())
    build(nc, *args)
    return _run(nc, [arrays], core_ids=[0]).results[0]["out_x"]
```

```python
import concourse.bass as bass
from concourse import mybir
from contextlib import ExitStack

B, S, C = 8, 128, 128
E = 8
R = 16
I = 512
H = 256
T = I // 128
HC = H // 128
OL = E * C // 128
OH = C // OL
HALF = B // 2
N = HALF * S
TOP_K = 2
SCALING = 32.0 / R
STOP_SCALE = 1.0 / 12
NSH = 2 * T
LOWEST = -3.0e38
_WIDTHS = [C, C, C, C, 1, 1, (2 * HC + 1) * E]
SMALL_PARTS = [(sum(_WIDTHS[:n]), width) for n, width in enumerate(_WIDTHS)]
SMALL = sum(_WIDTHS)
WARM = 8


def build(nc, x, cond, small, w1, shared, skill, layer3, out):
    fp32, fp32r, i32 = mybir.dt.float32, mybir.dt.float32r, mybir.dt.int32
    ALU, ACT, AX = mybir.AluOpType, mybir.ActivationFunctionType, mybir.AxisListType

    ctx = ExitStack()
    with ctx:
        def sb(name, shape, dt=fp32):
            return ctx.enter_context(nc.sbuf_tensor(name, shape, dt))

        def sem(name):
            return ctx.enter_context(nc.semaphore(name))

        ident = sb("ident", [128, 128])
        seg = sb("seg", [128, E])
        delta = sb("delta", [128, OH])
        rev = sb("rev", [128, E])
        condb = sb("condb", [128, B * E])
        segcond = sb("segcond", [128, B, E])
        wcol = sb("wcol", [128, B])
        mix1 = sb("mix1", [128, B, OH])
        m1 = sb("m1", [128, B])
        m2 = sb("m2", [128, B])
        eq = sb("eq", [128, B, E])
        val = sb("val", [128, B, E])
        rank = sb("rank", [128, TOP_K, B])
        hot1 = sb("hot1", [128, B, E])
        hot2 = sb("hot2", [128, B, E])
        rest = sb("rest", [128, B, E])
        chosen = sb("chosen", [128, B * TOP_K], i32)
        shifted = sb("shifted", [128, B, E])
        expo = sb("expo", [128, B, E])
        total = sb("total", [128, B])
        rtotal = sb("rtotal", [128, B])
        prob = sb("prob", [128, B, E])
        picked = sb("picked", [128, B, E])
        pk = sb("pk", [128, B, TOP_K])
        pksum = sb("pksum", [128, B])
        rpksum = sb("rpksum", [128, B])
        wnorm = sb("wnorm", [128, B, TOP_K])
        wpart = sb("wpart", [128, B, TOP_K])
        wsel = sb("wsel", [128, B * TOP_K])

        x_in = sb("x_in", [S, B, C])
        small_sb = sb("small_sb", [128, SMALL])
        a_sb, b_sb, base_t, mask_t, b0col, b1col, bias3 = (small_sb[:, at:at + n] for at, n in SMALL_PARTS)
        bias_t = bias3.rearrange("p (n e) -> p n e", e=E)
        warm = sb("warm", [128, 128])
        w1_sb = sb("w1_sb", [128, OL, C])
        p1 = sb("p1", [C, B, C])
        b_mix = sb("b_mix", [128, B, C])
        p0 = sb("p0", [C, B, C])
        x_t = sb("x_t", [C, B * S])
        x1_t = sb("x1_t", [C, B * S])
        x2_t = sb("x2_t", [C, B * S])
        x2s = sb("x2s", [C, B * S])
        shared_sb = sb("shared_sb", [128, 3, I])
        shared_h, shared_l = sb("shared_h", [128, 3, I], fp32r), sb("shared_l", [128, 3, I], fp32r)
        x2_h, x2_l = sb("x2_h", [C, B * S], fp32r), sb("x2_l", [C, B * S], fp32r)
        hid_h, hid_l = sb("hid_h", [128, 3, N], fp32r), sb("hid_l", [128, 3, N], fp32r)
        pair_w = sb("pair_w", [128, 2 * TOP_K, 3, I])
        gelu = sb("gelu", [128, 2, N])
        hid = sb("hid", [128, 2, N])
        w3 = sb("w3", [128, 2, 3, H])
        bias_hot = sb("bias_hot", [128, 2 * HC + 1, B, E])
        bsel = sb("bsel", [128, 2 * HC + 1, B])
        x3_t = sb("x3_t", [C, 2, S])
        x3b_t = sb("x3b_t", [C, 2, S])
        half3 = sb("half3", [128, HC, S])
        tanh3 = sb("tanh3", [128, HC, S])
        gate3 = sb("gate3", [128, HC, S])
        hid3 = sb("hid3", [128, HC, S])
        out_sb = sb("out_sb", [S, 2, C])

        bank = [ctx.enter_context(nc.psum_tensor(f"bank{n}", [128, 512], fp32)) for n in range(8)]
        g_ps, u_ps = bank[0:2], bank[2:4]
        shg_ps = [bank[0], bank[1], bank[6]]
        shu_ps = [bank[2], bank[3], bank[4]]
        acc_ps = bank[4]
        sh_acc = [bank[5], bank[7]]
        up3_ps = bank[7]

        cond_in, adapters_in, small_in = sem("cond_in"), sem("adapters_in"), sem("small_in")
        x_loaded = [sem("x_loaded0"), sem("x_loaded1")]
        w1_in = sem("w1_in")
        shared_in = [sem(f"shared_in{n}") for n in range(3)]
        sh_high, sh_low = sem("sh_high"), sem("sh_low")
        x2_high, x2_low, hid_high, hid_low = sem("x2_high"), sem("x2_low"), sem("hid_high"), sem("hid_low")
        pair_in = [sem(f"pair_in{n}") for n in range(2 * TOP_K)]
        w3_in = [sem(f"w3_in{n}") for n in range(2)]
        stored = [sem(f"stored{n}") for n in range(2)]
        pool_step = sem("pool_step")
        consts = sem("consts")
        delta_ready = sem("delta_ready")
        dve_step = sem("dve_step")
        mix_ready, routed, shifted_ready, expo_ready = sem("mix_ready"), sem("routed"), sem("shifted_ready"), sem("expo_ready")
        warm_ready = sem("warm_ready")
        xt_done, xt_ready = sem("xt_done"), sem("xt_ready")
        b_mixed, p0_done, p0_ready = sem("b_mixed"), sem("p0_done"), sem("p0_ready")
        p1_done, p1_ready = sem("p1_done"), sem("p1_ready")
        x1_done, x1_ready = sem("x1_done"), sem("x1_ready")
        x2_done, x2_ready = sem("x2_done"), sem("x2_ready")
        g_done, u_done, gelu_ready, hid_ready, down_done = (
            sem("g_done"), sem("u_done"), sem("gelu_ready"), sem("hid_ready"), sem("down_done"))
        x2s_ready = sem("x2s_ready")
        x3_ready, x3b_ready = sem("x3_ready"), sem("x3b_ready")
        up3_done, gate3_done, half3_ready, tanh3_ready, gate3_ready, hid3_ready = (
            sem("up3_done"), sem("gate3_done"), sem("half3_ready"), sem("tanh3_ready"), sem("gate3_ready"), sem("hid3_ready"))
        out_done, out_ready = sem("out_done"), sem("out_ready")

        def columns(b):
            return bass.DynSlice(b * S, S)

        def at_least(v, n):
            return not isinstance(v, int) or v >= n

        def is_last(b):
            return isinstance(b, int) and b == B - 1

        def out_bank(b):
            return bank[0] if is_last(b) else bank[6]

        def gate3_bank(b):
            return bank[1] if is_last(b) else bank[5]

        def fills(b, q):
            return (b - q) // 2 + 1

        block = ctx.enter_context(nc.Block())

        @block.sync
        def _(sp):
            sp.dma_start(condb[:, :], cond.rearrange("b e -> (b e)").partition_broadcast(128)).then_inc(cond_in, 16)
            for h in range(2):
                sp.dma_start(x_in[:, HALF * h:HALF * (h + 1), :],
                             x[HALF * h:HALF * (h + 1), :, :].rearrange("b s c -> s b c")).then_inc(x_loaded[h], 16)
            sp.dma_start(w1_sb[:, :, :], w1.rearrange("g (oh ol) t -> (g oh) ol t", ol=OL)).then_inc(w1_in, 16)
            for n in range(3):
                sp.dma_start(shared_sb[:, n, :], shared[:, n, :]).then_inc(shared_in[n], 16)
            sp.wait_ge(routed, 1)

            def load_pair(b, k, q, used=None):
                slot = TOP_K * q + k
                e = sp.value_load(chosen[0:1, bass.DynSlice(TOP_K * b + k, 1)], min_val=0, max_val=E - 1)
                if used is not None:
                    sp.wait_ge(down_done, used)
                sp.dma_start(pair_w[:, slot, :, :],
                             skill[bass.DynSlice(e, 1), :, :, :].rearrange("o p n i -> (o p) n i")).then_inc(pair_in[slot], 16)

            def load_w3(b, q, used=None):
                e = sp.value_load(chosen[0:1, bass.DynSlice(TOP_K * b, 1)], min_val=0, max_val=E - 1)
                if used is not None:
                    sp.wait_ge(out_done, used)
                sp.dma_start(w3[:, q, :, :], layer3[bass.DynSlice(e, 1), :, :, :].rearrange("o p n h -> (o p) n h")
                             ).then_inc(w3_in[q], 16)

            def store(b, q):
                sp.wait_ge(out_ready, b + 1)
                sp.dma_start(out[bass.DynSlice(b, 1), :, :].rearrange("o s c -> (o s) c"),
                             out_sb[:, q, :]).then_inc(stored[q], 16)

            def refill(b, q, first=True, second=True, before_last=True):
                if first:
                    load_pair(b + 1, 1, 1 - q, NSH + TOP_K * b)
                if before_last:
                    load_w3(b, q, b - 1)
                    store(b - 2, q)
                if second:
                    load_pair(b + 2, 0, q, NSH + TOP_K * b + 1)

            for b in range(2):
                for k in range(TOP_K):
                    load_pair(b, k, b)
                load_w3(b, b)
            refill(0, 0, first=False, before_last=False)
            refill(1, 1, before_last=False)
            with sp.Fori(1, B // 2 - 1) as j:
                for q in range(2):
                    refill(2 * j + q, q)
            refill(B - 2, 0, second=False)
            refill(B - 1, 1, first=False, second=False)
            store(B - 2, 0)
            store(B - 1, 1)
            for q in range(2):
                sp.wait_ge(stored[q], 16 * (B // 2))

        @block.gpsimd
        def _(pool):
            pool.memset(ident[:, :], 0.0).then_inc(pool_step, 1)
            pool.memset(seg[:, :], 1.0).then_inc(pool_step, 1)
            pool.wait_ge(pool_step, 2)
            pool.affine_select(out=ident[:, :], in_=ident[:, :], compare_op=ALU.not_equal, fill=1.0, base=0,
                               pattern=[[-1, 128]], channel_multiplier=1).then_inc(consts, 1)
            pool.affine_select(out=seg[:, :], in_=seg[:, :], compare_op=ALU.is_ge, fill=0.0, base=0,
                               pattern=[[-R, E]], channel_multiplier=1).then_inc(pool_step, 1)
            pool.wait_ge(pool_step, 3)
            pool.affine_select(out=seg[:, :], in_=seg[:, :], compare_op=ALU.is_ge, fill=0.0, base=R - 1,
                               pattern=[[R, E]], channel_multiplier=-1).then_inc(consts, 1)
            pool.iota(rev[:, :], [[-1, E]], base=E, channel_multiplier=0,
                      allow_small_or_imprecise_dtypes=True).then_inc(consts, 1)
            for n in range(3):
                pool.wait_ge(sh_high, n + 1)
                pool.tensor_tensor(shared_l[:, n, :], shared_sb[:, n, :], shared_h[:, n, :].bitcast(fp32),
                                   ALU.subtract).then_inc(sh_low, 1)
            for k in range(NSH):
                pool.wait_ge(hid_high, k + 1)
                pool.tensor_tensor(hid_l[:, k % 3, :], hid[:, k % 2, :], hid_h[:, k % 3, :].bitcast(fp32),
                                   ALU.subtract).then_inc(hid_low, 1)

        @block.scalar
        def _(act):
            act.dma_start(small_sb[:, 0:2 * C], small[:, 0:2 * C]).then_inc(adapters_in, 16)
            act.dma_start(small_sb[:, 2 * C:SMALL], small[:, 2 * C:SMALL]).then_inc(small_in, 16)
            for h in range(2):
                act.wait_ge(xt_done, h + 1)
                act.activation(x_t[:, N * h:N * (h + 1)], bank[h][:, :], ACT.Copy).then_inc(xt_ready, 1)
            act.wait_ge(shifted_ready, 1)
            act.activation(expo[:, :, :], shifted[:, :, :], ACT.Exp).then_inc(expo_ready, 1)
            for n in range(3):
                act.wait_ge(shared_in[n], 16)
                act.activation(shared_h[:, n, :], shared_sb[:, n, :], ACT.Copy).then_inc(sh_high, 1)
            act.preload_act_table(ACT.Gelu_apprx_tanh)

            def gelu_step(k, n, ps):
                act.wait_ge(g_done, k + 1)
                if at_least(k, 2):
                    act.wait_ge(hid_ready, k - 1)
                act.activation(gelu[:, n, :], ps[:, :], ACT.Gelu_apprx_tanh).then_inc(gelu_ready, 1)

            def copy_out(b, q):
                act.wait_ge(out_done, b + 1)
                if at_least(b, 2):
                    act.wait_ge(stored[q], 16 * (fills(b, q) - 1))
                act.activation(out_sb[:, q, :], out_bank(b)[:, 0:C], ACT.Copy).then_inc(out_ready, 1)

            def tanh_step(b, parts=1):
                n = HC // parts
                for c in range(parts):
                    act.wait_ge(half3_ready, HC * b + n * (c + 1))
                    act.activation(tanh3[:, n * c:n * (c + 1), :], half3[:, n * c:n * (c + 1), :],
                                   ACT.Tanh).then_inc(tanh3_ready, 1)

            def batch(b, q, last=True, before_last=True):
                gelu_step(NSH + TOP_K * b, 0, g_ps[0])
                if before_last:
                    copy_out(b - 2, q)
                gelu_step(NSH + TOP_K * b + 1, 1, g_ps[1])
                if last:
                    tanh_step(b - 1)

            def round_hidden(k):
                act.wait_ge(hid_ready, k + 1)
                if k >= 3:
                    act.wait_ge(down_done, k - 2)
                act.activation(hid_h[:, k % 3, :], hid[:, k % 2, :], ACT.Copy).then_inc(hid_high, 1)

            gelu_step(0, 0, shg_ps[0])
            for k in range(1, NSH):
                gelu_step(k, k % 2, shg_ps[k % 3])
                round_hidden(k - 1)
            round_hidden(NSH - 1)
            batch(0, 0, last=False, before_last=False)
            batch(1, 1, before_last=False)
            with act.Fori(1, B // 2) as j:
                for q in range(2):
                    batch(2 * j + q, q)
            tanh_step(B - 1, parts=HC)
            copy_out(B - 2, 0)
            copy_out(B - 1, 1)

        @block.vector
        def _(dve):
            steps = [0]

            def then(ins):
                steps[0] += 1
                ins.then_inc(dve_step, 1)
                dve.wait_ge(dve_step, steps[0])

            def over_e(a):
                return a.unsqueeze(2).broadcast_to([128, B, E])

            def over_b(a):
                return a.unsqueeze(1).broadcast_to([128, B, a.shape[1]])

            dve.memset(warm[:, :], 0.0).then_inc(warm_ready, 1)
            cond3 = condb[:, :].rearrange("p (b e) -> p b e", e=E)
            dve.wait_ge(consts, 1)
            dve.reduce_sum(delta[:, :], ident[:, :].rearrange("p (e j) -> p j e", j=OH), axis=AX.X).then_inc(delta_ready, 1)
            dve.wait_ge(cond_in, 16)
            dve.wait_ge(consts, 3)
            then(dve.tensor_tensor(segcond[:, :, :], cond3, over_b(seg[:, :]), ALU.mult))
            then(dve.reduce_sum(wcol[:, :], segcond[:, :, :], axis=AX.X))
            dve.wait_ge(adapters_in, 16)
            for h in range(2):
                bs = slice(HALF * h, HALF * (h + 1))
                dve.scalar_tensor_tensor(b_mix[:, bs, :], b_sb.unsqueeze(1).broadcast_to([128, HALF, C]), SCALING,
                                         wcol[:, bs].unsqueeze(2).broadcast_to([128, HALF, C]),
                                         ALU.mult, ALU.mult).then_inc(b_mixed, 1)
            dve.wait_ge(delta_ready, 1)
            dve.tensor_tensor(mix1[:, :, :], wcol[:, :].unsqueeze(2).broadcast_to([128, B, OH]),
                              over_b(delta[:, :]), ALU.mult).then_inc(mix_ready, 1)
            then(dve.reduce_max(m1[:, :], cond3, axis=AX.X))
            dve.tensor_tensor(shifted[:, :, :], cond3, over_e(m1[:, :]), ALU.subtract).then_inc(shifted_ready, 1)
            then(dve.tensor_tensor(eq[:, :, :], cond3, over_e(m1[:, :]), ALU.is_equal))
            then(dve.tensor_tensor(val[:, :, :], eq[:, :, :], over_b(rev[:, :]), ALU.mult))
            then(dve.reduce_max(rank[:, 0, :], val[:, :, :], axis=AX.X))
            then(dve.tensor_tensor(hot1[:, :, :], val[:, :, :], over_e(rank[:, 0, :]), ALU.is_equal))
            then(dve.scalar_tensor_tensor(rest[:, :, :], hot1[:, :, :], LOWEST, cond3, ALU.mult, ALU.add))
            dve.wait_ge(small_in, 16)

            def weights0(h):
                dve.wait_ge(p0_done, h + 1)
                dve.tensor_tensor(p0[:, HALF * h:HALF * (h + 1), :], bank[3 + h][:, :].rearrange("c (b o) -> c b o", o=C),
                                  base_t.unsqueeze(1).broadcast_to([C, HALF, C]), ALU.add).then_inc(p0_ready, 1)

            def weights1(h):
                dve.wait_ge(p1_done, h + 1)
                ols = slice(h * (OL // 2), (h + 1) * (OL // 2))
                dve.tensor_tensor(
                    p1[:, :, :].rearrange("t b (oh ol) -> t ol b oh", ol=OL)[:, ols, :, :],
                    bank[5 + h][:, :].rearrange("t (ol b oh) -> t ol b oh", b=B, oh=OH),
                    mask_t.rearrange("t (oh ol) -> t ol oh", ol=OL)[:, ols, :].unsqueeze(2)
                    .broadcast_to([128, OL // 2, B, OH]), ALU.mult).then_inc(p1_ready, 1)

            def stream1(h):
                dve.wait_ge(x1_done, h + 1)
                dve.wait_ge(xt_ready, h + 1)
                dve.scalar_tensor_tensor(x1_t[:, N * h:N * (h + 1)], bank[h][:, :], b0col,
                                         x_t[:, N * h:N * (h + 1)], ALU.add, ALU.add).then_inc(x1_ready, 1)

            def route_second():
                then(dve.reduce_max(m2[:, :], rest[:, :, :], axis=AX.X))
                then(dve.tensor_tensor(eq[:, :, :], rest[:, :, :], over_e(m2[:, :]), ALU.is_equal))
                then(dve.tensor_tensor(val[:, :, :], eq[:, :, :], over_b(rev[:, :]), ALU.mult))
                then(dve.reduce_max(rank[:, 1, :], val[:, :, :], axis=AX.X))
                dve.tensor_scalar(chosen[:, :].rearrange("p (b k) -> p k b", k=TOP_K), rank[:, :, :], -1.0, float(E),
                                  ALU.mult, ALU.add).then_inc(routed, 1)

            def stream2(h):
                dve.wait_ge(x2_done, h + 1)
                dve.wait_ge(x1_ready, h + 1)
                for dst, done in ((x2_h, x2_high), (x2_t, x2_ready)):
                    dve.scalar_tensor_tensor(dst[:, N * h:N * (h + 1)], bank[3 + h][:, :], b1col,
                                             x1_t[:, N * h:N * (h + 1)], ALU.add, ALU.add).then_inc(done, 1)

            def stream2_rest(h):
                dve.wait_ge(x2_ready, h + 1)
                dve.tensor_tensor(x2_l[:, N * h:N * (h + 1)], x2_t[:, N * h:N * (h + 1)],
                                  x2_h[:, N * h:N * (h + 1)].bitcast(fp32), ALU.subtract).then_inc(x2_low, 1)

            weights0(0)
            route_second()
            weights0(1)
            stream1(0)
            weights1(0)
            weights1(1)
            stream1(1)
            stream2(0)
            stream2_rest(0)
            stream2(1)

            def softmax():
                then(dve.tensor_tensor(hot2[:, :, :], val[:, :, :], over_e(rank[:, 1, :]), ALU.is_equal))
                dve.wait_ge(expo_ready, 1)
                then(dve.reduce_sum(total[:, :], expo[:, :, :], axis=AX.X))
                then(dve.reciprocal(rtotal[:, :], total[:, :]))
                then(dve.tensor_tensor(prob[:, :, :], expo[:, :, :], over_e(rtotal[:, :]), ALU.mult))

            def chosen_probabilities():
                for k, hot in enumerate((hot1, hot2)):
                    then(dve.tensor_tensor(picked[:, :, :], prob[:, :, :], hot[:, :, :], ALU.mult))
                    then(dve.reduce_sum(pk[:, :, k], picked[:, :, :], axis=AX.X))

            def expert_weights():
                then(dve.reduce_sum(pksum[:, :], pk[:, :, :], axis=AX.X))
                then(dve.reciprocal(rpksum[:, :], pksum[:, :]))
                then(dve.tensor_tensor(wnorm[:, :, :], pk[:, :, :],
                                       rpksum[:, :].unsqueeze(2).broadcast_to([128, B, TOP_K]), ALU.mult))
                then(dve.tensor_scalar(wpart[:, :, :], wnorm[:, :, :], 1.0 - STOP_SCALE, None, ALU.mult))
                then(dve.scalar_tensor_tensor(wsel[:, :].rearrange("p (b k) -> p b k", k=TOP_K), wnorm[:, :, :],
                                              STOP_SCALE, wpart[:, :, :], ALU.mult, ALU.add))

            def bias_columns():
                n = 2 * HC + 1
                then(dve.tensor_tensor(bias_hot[:, :, :, :], bias_t.unsqueeze(2).broadcast_to([128, n, B, E]),
                                       hot1[:, :, :].unsqueeze(1).broadcast_to([128, n, B, E]), ALU.mult))
                then(dve.reduce_sum(bsel[:, :, :], bias_hot[:, :, :, :], axis=AX.X))

            def hidden(k, n, weight=None):
                dve.wait_ge(gelu_ready, k + 1)
                dve.wait_ge(u_done, k + 1)
                if isinstance(k, int) and 2 <= k < NSH + 2:
                    dve.wait_ge(hid_low, k - 1)
                elif at_least(k, 2):
                    dve.wait_ge(down_done, k - 1)
                if weight is None:
                    dve.tensor_tensor(hid[:, n, :], gelu[:, n, :], shu_ps[k % 3][:, :], ALU.mult).then_inc(hid_ready, 1)
                else:
                    dve.scalar_tensor_tensor(hid[:, n, :], gelu[:, n, :], wsel[:, bass.DynSlice(weight, 1)],
                                             u_ps[n][:, :], ALU.mult, ALU.mult).then_inc(hid_ready, 1)

            def add_shared(h):
                dve.wait_ge(down_done, T * (h + 1))
                dve.tensor_tensor(x2s[:, N * h:N * (h + 1)], sh_acc[h][:, :], x2_t[:, N * h:N * (h + 1)],
                                  ALU.add).then_inc(x2s_ready, 1)

            def residual(b, q):
                dve.wait_ge(down_done, NSH + TOP_K * (b + 1))
                if at_least(b, 2):
                    dve.wait_ge(out_done, b - 1)
                dve.tensor_tensor(x3_t[:, q, :], acc_ps[:, 0:S], x2s[:, columns(b)], ALU.add).then_inc(x3_ready, 1)

            def residual_bias(b, q):
                dve.wait_ge(x3_ready, b + 1)
                dve.tensor_scalar(x3b_t[:, q, :], x3_t[:, q, :], bsel[:, 2 * HC, bass.DynSlice(b, 1)], None,
                                  ALU.add).then_inc(x3b_ready, 1)

            def halve3(b):
                dve.wait_ge(up3_done, b + 1)
                if at_least(b, 1):
                    dve.wait_ge(tanh3_ready, b)
                for c in range(HC):
                    dve.tensor_scalar(half3[:, c, :], up3_ps[:, S * c:S * (c + 1)], bsel[:, c, bass.DynSlice(b, 1)], 0.5,
                                      ALU.add, ALU.mult).then_inc(half3_ready, 1)

            def gated3(b):
                dve.wait_ge(half3_ready, HC * (b + 1))
                dve.wait_ge(gate3_done, b + 1)
                for c in range(HC):
                    dve.scalar_tensor_tensor(gate3[:, c, :], gate3_bank(b)[:, S * c:S * (c + 1)],
                                             bsel[:, HC + c, bass.DynSlice(b, 1)], half3[:, c, :],
                                             ALU.add, ALU.mult).then_inc(gate3_ready, 1)

            def silu_gate3(b, parts=1):
                dve.wait_ge(gate3_ready, HC * (b + 1))
                if at_least(b, 1):
                    dve.wait_ge(out_done, b)
                n = HC // parts
                for c in range(parts):
                    dve.wait_ge(tanh3_ready, b + 1 + c)
                    dve.scalar_tensor_tensor(hid3[:, n * c:n * (c + 1), :], tanh3[:, n * c:n * (c + 1), :], 1.0,
                                             gate3[:, n * c:n * (c + 1), :], ALU.add, ALU.mult).then_inc(hid3_ready, 1)

            def batch(b, q, last=True):
                hidden(NSH + TOP_K * b, 0, TOP_K * b)
                if last:
                    residual(b - 1, 1 - q)
                    residual_bias(b - 1, 1 - q)
                hidden(NSH + TOP_K * b + 1, 1, TOP_K * b + 1)
                if last:
                    halve3(b - 1)
                    gated3(b - 1)
                    silu_gate3(b - 1)

            between = {0: lambda: stream2_rest(1), 1: softmax, 2: chosen_probabilities, 3: expert_weights, 4: bias_columns,
                       5: lambda: add_shared(0)}
            for k in range(NSH):
                hidden(k, k % 2)
                if k in between:
                    between[k]()
            batch(0, 0, last=False)
            add_shared(1)
            batch(1, 1)
            with dve.Fori(1, B // 2 - 1) as j:
                for q in range(2):
                    batch(2 * j + q, q)
            batch(B - 2, 0)
            hidden(NSH + TOP_K * (B - 1), 0, TOP_K * (B - 1))
            residual(B - 2, 0)
            residual_bias(B - 2, 0)
            hidden(NSH + TOP_K * (B - 1) + 1, 1, TOP_K * (B - 1) + 1)
            halve3(B - 2)
            residual(B - 1, 1)
            gated3(B - 2)
            silu_gate3(B - 2)
            halve3(B - 1)
            residual_bias(B - 1, 1)
            gated3(B - 1)
            silu_gate3(B - 1, parts=HC)

        @block.tensor
        def _(pe):
            pe.wait_ge(warm_ready, 1)
            for _ in range(WARM):
                pe.matmul(bank[6][:, 0:128], warm[:, :], warm[:, :], start=True, stop=True)
            pe.wait_ge(consts, 1)

            def turn_x(h):
                pe.wait_ge(x_loaded[h], 16)
                for n in range(HALF):
                    mm = pe.transpose(bank[h][:, S * n:S * (n + 1)], x_in[:, HALF * h + n, :], ident[:, :])
                mm.then_inc(xt_done, 1)

            def mix0(h):
                pe.wait_ge(adapters_in, 16)
                pe.wait_ge(b_mixed, h + 1)
                pe.matmul(bank[3 + h][:, :], a_sb, b_mix[:, HALF * h:HALF * (h + 1), :].rearrange("p b o -> p (b o)"),
                          start=True, stop=True).then_inc(p0_done, 1)

            def mix1_part(h):
                pe.wait_ge(mix_ready, 1)
                pe.wait_ge(w1_in, 16)
                for a in range(OL // 2):
                    mm = pe.matmul(bank[5 + h][:, 128 * a:128 * (a + 1)], w1_sb[:, h * (OL // 2) + a, :],
                                   mix1[:, :, :].rearrange("p b j -> p (b j)"), start=True, stop=True)
                mm.then_inc(p1_done, 1)

            def product0(h):
                pe.wait_ge(p0_ready, h + 1)
                pe.wait_ge(xt_ready, h + 1)
                for n in range(HALF):
                    b = HALF * h + n
                    mm = pe.matmul(bank[h][:, S * n:S * (n + 1)], p0[:, b, :], x_t[:, columns(b)], start=True, stop=True)
                mm.then_inc(x1_done, 1)

            def product1(h):
                pe.wait_ge(p1_ready, 2)
                pe.wait_ge(x1_ready, h + 1)
                for n in range(HALF):
                    b = HALF * h + n
                    mm = pe.matmul(bank[3 + h][:, S * n:S * (n + 1)], p1[:, b, :], x1_t[:, columns(b)],
                                   start=True, stop=True)
                mm.then_inc(x2_done, 1)

            turn_x(0)
            mix0(0)
            turn_x(1)
            mix0(1)
            product0(0)
            mix1_part(0)
            mix1_part(1)
            product0(1)
            product1(0)
            product1(1)

            shared_products = ((shg_ps, g_done), (shu_ps, u_done))

            def shared_high(k, m):
                h, t, n = k // T, k % T, k % 3
                ps, _ = shared_products[m]
                if k >= 3:
                    pe.wait_ge(hid_ready, k - 2)
                if k in (1, 2):
                    pe.wait_ge(x2_ready, k)
                if t == 0:
                    pe.wait_ge(x2_high, h + 1)
                if k == 0:
                    pe.wait_ge(sh_high, m + 1)
                    pe.wait_ge(sh_low, m + 1)
                high = x2_h[:, N * h:N * (h + 1)]
                pe.matmul(ps[n][:, :], shared_h[:, m, 128 * t:128 * (t + 1)], high, start=True, stop=False)
                pe.matmul(ps[n][:, :], shared_l[:, m, 128 * t:128 * (t + 1)], high, start=False, stop=False)

            def shared_low(k, m):
                h, t, n = k // T, k % T, k % 3
                ps, done = shared_products[m]
                if t == 0:
                    pe.wait_ge(x2_low, h + 1)
                pe.matmul(ps[n][:, :], shared_h[:, m, 128 * t:128 * (t + 1)], x2_l[:, N * h:N * (h + 1)],
                          start=False, stop=True).then_inc(done, 1)

            def shared_down(k):
                h, t, n = k // T, k % T, k % 3
                if k == 0:
                    pe.wait_ge(sh_low, 3)
                pe.wait_ge(hid_high, k + 1)
                pe.matmul(sh_acc[h][:, :], shared_h[:, 2, C * t:C * (t + 1)], hid_h[:, n, :], start=(t == 0), stop=False)
                pe.matmul(sh_acc[h][:, :], shared_l[:, 2, C * t:C * (t + 1)], hid_h[:, n, :], start=False, stop=False)
                pe.wait_ge(hid_low, k + 1)
                pe.matmul(sh_acc[h][:, :], shared_h[:, 2, C * t:C * (t + 1)], hid_l[:, n, :], start=False, stop=(t == T - 1)
                          ).then_inc(down_done, 1)

            def gate_up(b, k, q):
                slot, step = TOP_K * q + k, NSH + TOP_K * b + k
                pe.wait_ge(pair_in[slot], 16 * fills(b, q))
                pe.wait_ge(hid_ready, step - 1)
                for n, (ps, done) in enumerate(((g_ps[k], g_done), (u_ps[k], u_done))):
                    for t in range(T):
                        mm = pe.matmul(ps[:, S * t:S * (t + 1)], pair_w[:, slot, n, 128 * t:128 * (t + 1)], x2_t[:, columns(b)],
                                       start=True, stop=True)
                    mm.then_inc(done, 1)

            def down(b, k, q):
                slot, step = TOP_K * q + k, NSH + TOP_K * b + k
                pe.wait_ge(hid_ready, step + 1)
                if k == 0 and at_least(b, 1):
                    pe.wait_ge(x3_ready, b)
                for t in range(T):
                    mm = pe.matmul(acc_ps[:, 0:S], pair_w[:, slot, 2, C * t:C * (t + 1)], hid[:, k, S * t:S * (t + 1)],
                                   start=(k == 0 and t == 0), stop=(k == TOP_K - 1 and t == T - 1))
                mm.then_inc(down_done, 1)

            def product3(b, q, n):
                pe.wait_ge(w3_in[q], 16 * fills(b, q))
                pe.wait_ge(x3_ready, b + 1)
                if not at_least(b, 1):
                    pe.wait_ge(x2s_ready, 2)
                elif n == 0 or not is_last(b):
                    pe.wait_ge((half3_ready, gate3_ready)[n], HC * b)
                ps, done = ((up3_ps, up3_done), (gate3_bank(b), gate3_done))[n]
                for c in range(HC):
                    mm = pe.matmul(ps[:, S * c:S * (c + 1)], w3[:, q, n, 128 * c:128 * (c + 1)],
                                   x3_t[:, q, :], start=True, stop=True)
                mm.then_inc(done, 1)

            def up_gate3(b, q):
                product3(b, q, 0)
                product3(b, q, 1)

            def down3(b, q, parts=1):
                pe.wait_ge(x3b_ready, b + 1)
                if at_least(b, 1) and not is_last(b):
                    pe.wait_ge(out_ready, b)
                out_ps = out_bank(b)
                pe.matmul(out_ps[:, 0:C], x3b_t[:, q, :], ident[:, :], is_transpose=True, start=True, stop=False)
                for c in range(HC):
                    if c % (HC // parts) == 0:
                        pe.wait_ge(hid3_ready, b + 1 + c * parts // HC)
                    mm = pe.matmul(out_ps[:, 0:C], hid3[:, c, :], w3[:, q, 2, C * c:C * (c + 1)],
                                   start=False, stop=(c == HC - 1))
                mm.then_inc(out_done, 1)

            def batch(b, q, last=True, before_last=True):
                gate_up(b, 0, q)
                if last:
                    down(b - 1, 1, 1 - q)
                if before_last:
                    down3(b - 2, q)
                gate_up(b, 1, q)
                if last:
                    up_gate3(b - 1, 1 - q)
                down(b, 0, q)

            shared_high(0, 0)
            shared_high(0, 1)
            shared_high(1, 0)
            shared_low(0, 0)
            shared_low(0, 1)
            shared_high(1, 1)
            shared_low(1, 0)
            shared_low(1, 1)
            for k in range(2, NSH):
                for part in (shared_high, shared_low):
                    for m in range(2):
                        part(k, m)
                if k >= 3:
                    shared_down(k - 3)
            gate_up(0, 0, 0)
            shared_down(NSH - 3)
            gate_up(0, 1, 0)
            shared_down(NSH - 2)
            shared_down(NSH - 1)
            down(0, 0, 0)
            batch(1, 1, before_last=False)
            with pe.Fori(1, B // 2 - 1) as j:
                for q in range(2):
                    batch(2 * j + q, q)
            batch(B - 2, 0)
            gate_up(B - 1, 0, 1)
            down(B - 2, 1, 0)
            down3(B - 3, 1)
            gate_up(B - 1, 1, 1)
            down(B - 1, 0, 1)
            product3(B - 2, 0, 0)
            down(B - 1, 1, 1)
            product3(B - 2, 0, 1)
            up_gate3(B - 1, 1)
            down3(B - 2, 0)
            down3(B - 1, 1, parts=HC)


def kernel(**inputs):
    import numpy as _np
    import concourse.bacc as _bacc
    from concourse import mybir as _mybir
    from concourse.bass_utils import run_bass_kernel_spmd as _run

    def of(name):
        return _np.asarray(inputs[name])

    def gated(gate, up, down):
        lead = gate.shape[:-2]
        down = _np.swapaxes(down.reshape(*lead, T, 128, C), -3, -2).reshape(*lead, 128, I)
        return _np.stack([gate, up, down], axis=-2)

    up3, gate3 = (_np.swapaxes(of(name), 1, 2) for name in ("L3_cond_W_up", "L3_cond_W_gate"))
    down3 = of("L3_cond_W_down").reshape(E, C, HC, 128).transpose(0, 3, 2, 1).reshape(E, 128, H)
    bias3 = _np.concatenate([of("L3_cond_b_up").reshape(E, HC, 128), of("L3_cond_b_gate").reshape(E, HC, 128),
                             of("L3_cond_b_down").reshape(E, 1, 128)], axis=1)
    arrays = {
        "in_x": of("x"),
        "in_cond": of("cond_8"),
        "in_small": _np.concatenate([
            of("L0_cond_As").reshape(128, C), _np.swapaxes(of("L0_cond_Bs"), 1, 2).reshape(128, C),
            of("L0_cond_W_base").T, of("L1_cond_mask").T, of("L0_cond_b_base").reshape(C, 1),
            of("L1_cond_bias").reshape(C, 1), bias3.transpose(2, 1, 0).reshape(128, -1)], axis=1),
        "in_w1": of("L1_cond_weight"),
        "in_shared": gated(of("L2_cond_shared_gate"), of("L2_cond_shared_up"), of("L2_cond_shared_down")),
        "in_skill": gated(of("L2_cond_skill_gate"), of("L2_cond_skill_up"), of("L2_cond_skill_down")),
        "in_layer3": _np.stack([up3, gate3, down3], axis=2),
    }
    nc = _bacc.Bacc("TRN2", target_bir_lowering=False, num_devices=1)
    args = []
    for name, a in arrays.items():
        arrays[name] = _np.ascontiguousarray(a)
        args.append(nc.dram_tensor(name, a.shape, _mybir.dt.from_np(a.dtype), kind="ExternalInput").ap())
    args.append(nc.dram_tensor("out_x", (B, S, C), _mybir.dt.float32, kind="ExternalOutput").ap())
    build(nc, *args)
    return _run(nc, [arrays], core_ids=[0]).results[0]["out_x"]
```
